# Optimizing a Trainium2 kernel written in Bass

```python
import numpy as np
import jax
import jax.numpy as jnp

def _softmax(x, axis=-1):
    return jax.nn.softmax(x, axis=axis)

def _gelu(x):
    return jax.nn.gelu(x, approximate=True)

def _silu(x):
    return jax.nn.silu(x)

def _sigmoid(x):
    return jax.nn.sigmoid(x)

def _layernorm(x, axis=-1, eps=1e-05):
    m = jnp.mean(x, axis=axis, keepdims=True)
    v = jnp.var(x, axis=axis, keepdims=True)
    return (x - m) / jnp.sqrt(v + eps)

def _scatter_add(tgt, idx, src, axis=0):
    return tgt.at[idx].add(src)

def _segment_sum(src, seg, n):
    return jax.ops.segment_sum(src, seg, n)
kernel_name = 'mk_flamingo_gated_d1_seqx_r4_59f3fa'

def setup_inputs(seed: int=0):
    np.random.seed(seed)
    _w = jnp.asarray

    def _rec_inputs():
        import jax
        import jax.numpy as jnp
        _rk = jax.random.key(seed)
        x = -7.109e-05 + 0.9999 * jax.random.normal(jax.random.fold_in(_rk, 1), (4, 512, 512), jnp.float32)
        _lenS = 512 - jax.random.randint(jax.random.fold_in(_rk, 7), (4,), 0, max(1, 512 // 4) + 1, jnp.int32)
        _lenS2 = 512 - jax.random.randint(jax.random.fold_in(_rk, 8), (4,), 0, max(1, 512 // 4) + 1, jnp.int32)
        _ctx_512P = jax.random.normal(jax.random.fold_in(_rk, 11), (4, 16, 128), jnp.float32)
        _ctx_512c = jax.random.dirichlet(jax.random.fold_in(_rk, 511), 0.3 * jnp.ones((16,), jnp.float32), (4, 512))
        _ctx_512t = jnp.einsum('bsk,bkd->bsd', _ctx_512c, _ctx_512P)
        _ctx_512t = _ctx_512t * jax.lax.rsqrt(jnp.mean(jnp.square(_ctx_512t)) + 1e-12) * 0.953939
        ctx_512 = 2.81802e-05 + 1.00001 * (_ctx_512t + 0.3 * jax.random.normal(jax.random.fold_in(_rk, 611), (4, 512, 128), jnp.float32))
        _g = jax.random.normal(jax.random.fold_in(_rk, 9001), (2, 1), jnp.float32)
        _g = jnp.sign(_g) * jnp.maximum(jnp.abs(_g), 1.0) + (_g == 0) * 1.0
        g_xattn = _g[0]
        g_ffn = _g[1]
        return (x, ctx_512, g_xattn, g_ffn)
    x, ctx_512, g_xattn, g_ffn = _rec_inputs()

    def _L0_xattn_setup():
        import jax, jax.numpy as jnp
        import numpy as np
        EPS = 1e-06
        IMAGE_DIMS = 512
        key = jax.random.key(seed)
        k1, k2, k3 = jax.random.split(key, 3)
        B, I, J, D = (16, 512, 512, 128)
        p = jax.random.normal(k1, (B, I, J), dtype=jnp.float32)
        k_v = jax.random.normal(k2, (B, J, D), dtype=jnp.float32)
        W_k = jax.random.normal(k3, (D, D), dtype=jnp.float32) * (1.0 / np.sqrt(D))
        b_k = jnp.zeros((D,), dtype=jnp.float32)
        ln_gamma = jnp.ones((J,), dtype=jnp.float32)
        ln_beta = jnp.zeros((J,), dtype=jnp.float32)
        return {'p': p, 'k_v': k_v, 'W_k': W_k, 'b_k': b_k, 'ln_gamma': ln_gamma, 'ln_beta': ln_beta}
    _L0_xattn_all = _L0_xattn_setup()
    _L0_xattn_in = {k: v for k, v in _L0_xattn_all.items() if k in ('W_k', 'b_k', 'ln_gamma', 'ln_beta')}
    del _L0_xattn_all

    def _L0_ffn_setup():
        import jax, jax.numpy as jnp
        import numpy as np
        B, S, H = (2, 512, 512)
        E, I = (32, 256)
        SI = 1024
        K = 4
        G = 4
        TKG = 2
        SCALE = 2.5

        def _relu2(v):
            r = jax.nn.relu(v)
            return r * r
        key = jax.random.key(seed)
        ks = jax.random.split(key, 7)
        w = 0.02
        return {'x': jax.random.normal(ks[0], (B, S, H), jnp.float32), 'gate_w': jax.random.normal(ks[1], (H, E), jnp.float32) * w, 'e_bias': jax.random.normal(ks[2], (E,), jnp.float32) * 0.01, 'Wu': jax.random.normal(ks[3], (E, H, I), jnp.float32) * w, 'Wd': jax.random.normal(ks[4], (E, I, H), jnp.float32) * w, 'Wsu': jax.random.normal(ks[5], (H, SI), jnp.float32) * w, 'Wsd': jax.random.normal(ks[6], (SI, H), jnp.float32) * w}
    _L0_ffn_all = _L0_ffn_setup()
    _L0_ffn_in = {k: v for k, v in _L0_ffn_all.items() if k in ('gate_w', 'e_bias', 'Wu', 'Wd', 'Wsu', 'Wsd')}
    del _L0_ffn_all
    return {'x': x, 'ctx_512': ctx_512, 'g_xattn': g_xattn, 'g_ffn': g_ffn, 'L0_xattn_W_k': _L0_xattn_in['W_k'], 'L0_xattn_b_k': _L0_xattn_in['b_k'], 'L0_xattn_ln_gamma': _L0_xattn_in['ln_gamma'], 'L0_xattn_ln_beta': _L0_xattn_in['ln_beta'], 'L0_ffn_gate_w': _L0_ffn_in['gate_w'], 'L0_ffn_e_bias': _L0_ffn_in['e_bias'], 'L0_ffn_Wu': _L0_ffn_in['Wu'], 'L0_ffn_Wd': _L0_ffn_in['Wd'], 'L0_ffn_Wsu': _L0_ffn_in['Wsu'], 'L0_ffn_Wsd': _L0_ffn_in['Wsd']}

def reference(x, ctx_512, g_xattn, g_ffn, L0_xattn_W_k, L0_xattn_b_k, L0_xattn_ln_gamma, L0_xattn_ln_beta, L0_ffn_gate_w, L0_ffn_e_bias, L0_ffn_Wu, L0_ffn_Wd, L0_ffn_Wsu, L0_ffn_Wsd):
    import jax
    import jax.numpy as jnp

    def _L0_xattn_ref(p, k_v, W_k, b_k, ln_gamma, ln_beta):
        import jax, jax.numpy as jnp
        import numpy as np
        EPS = 1e-06
        IMAGE_DIMS = 512
        kv = k_v @ W_k.T + b_k
        out = jnp.einsum('bij,bjd->bid', p, kv)
        scale = IMAGE_DIMS ** (-0.5)
        sim = jnp.einsum('bid,bjd->bij', out, kv) * scale
        mu = jnp.mean(sim, axis=-1, keepdims=True)
        var = jnp.var(sim, axis=-1, keepdims=True)
        sim = (sim - mu) * jax.lax.rsqrt(var + EPS) * ln_gamma + ln_beta
        attn = jax.nn.softmax(sim, axis=-1)
        return attn

    def _L0_ffn_ref(x, gate_w, e_bias, Wu, Wd, Wsu, Wsd):
        import jax, jax.numpy as jnp
        import numpy as np
        B, S, H = (2, 512, 512)
        E, I = (32, 256)
        SI = 1024
        K = 4
        G = 4
        TKG = 2
        SCALE = 2.5

        def _relu2(v):
            r = jax.nn.relu(v)
            return r * r
        orig_shape = x.shape
        h = x.reshape(-1, H)
        T = h.shape[0]
        logits = h @ gate_w
        scores = jax.nn.sigmoid(logits)
        sfc = scores + e_bias[None, :]
        per_group = sfc.reshape(T, G, E // G)
        group_scores = jnp.sum(jax.lax.top_k(per_group, 2)[0], axis=-1)
        _, gidx = jax.lax.top_k(group_scores, TKG)
        group_mask = jnp.sum(jax.nn.one_hot(gidx, G, dtype=sfc.dtype), axis=1)
        score_mask = jnp.repeat(group_mask, E // G, axis=-1)
        sfc_masked = jnp.where(score_mask > 0, sfc, 0.0)
        _, topk_idx = jax.lax.top_k(sfc_masked, K)
        topk_w = jnp.take_along_axis(scores, topk_idx, axis=1)
        topk_w = topk_w / (jnp.sum(topk_w, axis=-1, keepdims=True) + 1e-20)
        topk_w = topk_w * SCALE
        combine = jnp.zeros((T, E), scores.dtype).at[jnp.arange(T)[:, None], topk_idx].add(topk_w)
        up = jnp.einsum('th,ehi->tei', h, Wu)
        act = _relu2(up)
        routed = jnp.einsum('tei,te,eih->th', act, combine, Wd)
        shared = _relu2(h @ Wsu) @ Wsd
        out = (routed + shared).reshape(orig_shape)
        return out
    x = x + jnp.tanh(g_xattn[0]) * _L0_xattn_ref(_layernorm(x, axis=-1), ctx_512, L0_xattn_W_k, L0_xattn_b_k, L0_xattn_ln_gamma, L0_xattn_ln_beta)
    x = x + jnp.tanh(g_ffn[0]) * _L0_ffn_ref(_layernorm(x, axis=-1), L0_ffn_gate_w, L0_ffn_e_bias, L0_ffn_Wu, L0_ffn_Wd, L0_ffn_Wsu, L0_ffn_Wsd)
    return x

_drawn_inputs = setup_inputs


def setup_inputs(seed=0):
    import zlib

    import numpy as np

    out = dict(_drawn_inputs(seed))
    spreads = {'L0_xattn_b_k': (0.0, 0.8),
     'L0_xattn_ln_gamma': (1.0, 0.6),
     'L0_xattn_ln_beta': (0.0, 0.8)}
    factors = {'ctx_512': 8.0, 'L0_xattn_W_k': 8.0}
    for name, (base, spread) in spreads.items():
        noise = np.random.default_rng([zlib.crc32(name.encode()), seed]).standard_normal(out[name].shape)
        drawn = base * np.exp(spread * noise) if base else spread * noise
        out[name] = jnp.asarray(drawn.astype(out[name].dtype))
    for name, factor in factors.items():
        out[name] = (out[name] * factor).astype(out[name].dtype)
    return out
```

```python
from contextlib import ExitStack

import concourse.bass as bass
from concourse import mybir

P = 128
N_BATCH, SEQ, H = 4, 512, 512
DC = 128
TPB = SEQ // P
NT = N_BATCH * TPB
HB = H // P
E, INNER = 32, 256
IB = INNER // P
SI = 1024
SB = SI // P
TOPK, GROUPS, TOP_GROUPS, SCALE = 4, 4, 2, 2.5
EG = E // GROUPS
UNROLL = 4
N_TILES = -(-((NT * P * TOPK + E * (P - 1)) // P) // UNROLL) * UNROLL
W_SLOTS = 4
FAR = -1.0e30


def block_kernel(nc, x, ctx_in, g_xattn, g_ffn, w_k, b_k, ln_gamma, ln_beta,
                 gate_w, e_bias, w_up, w_down, w_sh_up, w_sh_down, out):
    f32, i32, u32 = mybir.dt.float32, mybir.dt.int32, mybir.dt.uint32
    f16, bf16 = mybir.dt.float16, mybir.dt.bfloat16
    ALU, ACT, AX = mybir.AluOpType, mybir.ActivationFunctionType, mybir.AxisListType
    ds = bass.ds

    with ExitStack() as stack:
        def sb(name, shape, dt=f32):
            return stack.enter_context(nc.sbuf_tensor(name, shape, dt))

        def bank(name):
            return stack.enter_context(nc.psum_tensor(name, [P, 512], f32))

        def sem(name):
            return stack.enter_context(nc.semaphore(name))

        h_dram = nc.dram_tensor("h_rows", (NT * P, H), f32).ap()
        y_dram = nc.dram_tensor("y_rows", (N_TILES * P, H), f32).ap()

        X = sb("X", [P, NT, H])
        X2 = X[:, :, :].rearrange("p t n -> p (t n)")
        HR = sb("HR", [P, TPB, H])
        hT = sb("hT", [P, 2, HB, SEQ])
        hT2 = hT[:, :, :, :].rearrange("p s h n -> p (s h n)")
        wk = sb("wk", [P, DC])
        wkT = sb("wkT", [P, DC])
        bk = sb("bk", [DC, 1])
        g_raw = sb("g_raw", [P, 2])
        g_tanh = sb("g_tanh", [P, 2])
        gate = sb("gate", [P, HB, E])
        ebias = sb("ebias", [P, E])
        wsu = sb("wsu", [P, HB, SI])
        wsd = sb("wsd", [P, SB, H])
        rel = sb("rel", [P, 2, SEQ])
        act = sb("act", [P, 2, SEQ])
        lgT = sb("lgT", [E, SEQ])
        LG = sb("LG", [P, NT, E])
        LG2 = LG[:, :, :].rearrange("p t e -> p (t e)")
        bst = sb("bst", [P, TPB, 6])
        mv = sb("mv", [P, TPB, 2])
        veps = sb("veps", [P, TPB])
        rstd = sb("rstd", [P, 3, TPB])
        nmax = sb("nmax", [P, TPB])
        esum = sb("esum", [P, TPB])
        ecoef = sb("ecoef", [P, TPB])
        ident = sb("ident", [P, P])
        mhalf = sb("mhalf", [P, TPB])
        lower = sb("lower", [P, P], bf16)
        ones = sb("ones", [P, P], bf16)
        zeros = sb("zeros", [P, P], f16)
        iota_i = sb("iota_i", [P, P], i32)
        iota_f = sb("iota_f", [P, P])
        iota_h = sb("iota_h", [P, P], f16)
        part_i = sb("part_i", [P, 1], i32)
        part_f = sb("part_f", [P, 1])
        tok_i = sb("tok_i", [P, NT], i32)
        tok_f = sb("tok_f", [P, NT])
        lt44 = sb("lt44", [P, GROUPS, GROUPS])
        edge = sb("edge", [P, NT])
        sc = sb("sc", [P, NT, E])
        sfc = sb("sfc", [P, NT, E])
        sm = sb("sm", [P, NT, E])
        gsm = sb("gsm", [P, 6, NT * GROUPS])
        gcmp = sb("gcmp", [P, 2, NT, GROUPS, GROUPS])
        top8 = sb("top8", [P, NT, 8])
        idx8 = sb("idx8", [P, NT, 8], u32)
        idxf = sb("idxf", [P, NT, TOPK])
        chosen = sb("chosen", [P, NT, E], bf16)
        w4 = sb("w4", [P, NT * TOPK])
        wsum = sb("wsum", [P, NT])
        pre = sb("pre", [P, NT + 1, E])
        n_tl = sb("n_tl", [P, E])
        tend = sb("tend", [P, E])
        base = sb("base", [P, E])
        onesE = sb("onesE", [P, E])
        s4 = sb("s4", [P, NT * TOPK])
        s4i = sb("s4i", [P, NT * TOPK], u32)
        sp_i = sb("sp_i", [P, 2, NT * TOPK], u32)
        sp_f = sb("sp_f", [P, 2, NT * TOPK])
        eid = sb("eid", [P, 4])
        eid_i = sb("eid_i", [P, 2], i32)
        tab = sb("tab", [1, 2 * P], i32)
        done_tab = sb("done_tab", [1, E], i32)
        selA = sb("selA", [P, 2, TOPK, P], f16)
        selB = sb("selB", [P, 2, TOPK, N_TILES], f16)
        idx_g = sb("idx_g", [P, N_TILES], u32)
        idx_now = sb("idx_now", [P, UNROLL], u32)
        wu = sb("wu", [P, W_SLOTS, HB, INNER])
        wd = sb("wd", [P, W_SLOTS, IB, H])
        wu2 = wu[:, :, :, :].rearrange("p s h n -> p (s h n)")
        wd2 = wd[:, :, :, :].rearrange("p s h n -> p (s h n)")
        with ExitStack() as attention:
            def at(name, shape):
                return attention.enter_context(nc.sbuf_tensor(name, shape, f32))

            ctx_b = at("ctx_b", [P, TPB, DC])
            ctxT = at("ctxT", [DC, SEQ])
            kvT = at("kvT", [DC, SEQ])
            kv = at("kv", [P, TPB, DC])
            PS = at("PS", [P, TPB, SEQ])
            pT = at("pT", [P, TPB, SEQ])
            outT = at("outT", [DC, SEQ])
            t1 = at("t1", [P, 2, SEQ])
            t2 = at("t2", [P, 2, SEQ])
            ex = at("ex", [P, 2, SEQ])
            gam = at("gam", [P, SEQ])
            bet = at("bet", [P, SEQ])
        xg = sb("xg", [P, UNROLL, H])
        xgT = sb("xgT", [P, 2, HB, P])
        erel = sb("erel", [P, 2, INNER])
        eact = sb("eact", [P, 2, INNER])
        eactT = sb("eactT", [P, 2, IB, P])
        yb = sb("yb", [P, UNROLL, H])
        with ExitStack() as routing:
            tmp = routing.enter_context(nc.sbuf_tensor("tmp", [P, NT, TOPK, E], f32))
            oneh = routing.enter_context(nc.sbuf_tensor("oneh", [P, NT, TOPK, E], f32))
        yg = sb("yg", [P, 2, TOPK, H])
        yidx = sb("yidx", [P, 2, TOPK], u32)

        T = [bank("T0"), bank("T1")]
        U = [bank("U0"), bank("U1")]
        D = [bank("D0"), bank("D1"), bank("D2"), bank("D3")]

        names = """d_small d_x d_ctx d_w d_h d_out
            pool_c pool_r pool_idx pool_cidx
            dve_v dve_p dve_kv dve_pT dve_z dve_e dve_x1 dve_h dve_act dve_sh dve_hT dve_lg dve_ch
            dve_M dve_slot dve_tab dve_sel dve_cr dve_tabT dve_idx dve_eact dve_eT dve_y dve_out dve_cmb
            act_c act_ctxT act_kvT act_pT act_outT act_sim act_e act_r act_hT act_lgT act_sc act_xT act_er
            pe_wk pe_ctxT pe_kvT pe_kv pe_pT pe_outT pe_sim pe_up pe_down pe_hT pe_lgT pe_lg pe_rank
            pe_sel pe_tab pe_ix pe_xT pe_eu pe_eT pe_ed
            sp_w""".split()
        s = {n: sem(n) for n in names}
        d_wt = [sem(f"d_wt{i}") for i in range(W_SLOTS)]
        d_xg = [sem(f"d_xg{i}") for i in range(UNROLL)]
        d_y = [sem(f"d_y{i}") for i in range(UNROLL)]
        d_yg = [sem(f"d_yg{i}") for i in range(2)]

        def wait(eng, name, n):
            eng.wait_ge(s[name], n)

        def wait_first(eng, name, n):
            eng.wait_ge(s["pool_c"], 1)
            eng.wait_ge(s[name], n)

        gate_v = sb("gate_v", [P, 1])
        gate_p = sb("gate_p", [1, 1])

        def gate_pool(pool, name, n):
            wait(pool, name, n)
            pool.tensor_tensor(gate_p[:, :], mhalf[0:1, 0:1], mhalf[0:1, 0:1], ALU.add)

        blk = stack.enter_context(nc.Block())

        @blk.sync
        def _(sp):
            small = [(wk[:, :], w_k), (bk[:, :], b_k.rearrange("(p a) -> p a", a=1)),
                     (gam[:, :], ln_gamma.rearrange("(a n) -> a n", a=1).broadcast_to([P, SEQ])),
                     (bet[:, :], ln_beta.rearrange("(a n) -> a n", a=1).broadcast_to([P, SEQ])),
                     (g_raw[:, 0:1], g_xattn.rearrange("(a n) -> a n", a=1).broadcast_to([P, 1])),
                     (g_raw[:, 1:2], g_ffn.rearrange("(a n) -> a n", a=1).broadcast_to([P, 1])),
                     (ebias[:, :], e_bias.rearrange("(a n) -> a n", a=1).broadcast_to([P, E])),
                     (gate[:, :, :], gate_w.rearrange("(h p) e -> p h e", p=P))]
            x_rows = x.rearrange("b (t p) n -> p (b t) n", p=P)
            ctx_rows = ctx_in.rearrange("b (t p) n -> p (b t) n", p=P)
            h_rows = h_dram.rearrange("(t p) n -> p t n", p=P)
            sp.dma_start(X[:, 0:TPB, :], x_rows[:, 0:TPB, :]).then_inc(s["d_x"], 16)
            sp.dma_start(ctx_b[:, :, :], ctx_rows[:, 0:TPB, :]).then_inc(s["d_ctx"], 16)
            for dst, src in small:
                sp.dma_start(dst, src).then_inc(s["d_small"], 16)
            sp.dma_start(wsu[:, :, :], w_sh_up.rearrange("(h p) n -> p h n", p=P)).then_inc(s["d_w"], 16)
            sp.dma_start(wsd[:, :, :], w_sh_down.rearrange("(k p) n -> p k n", p=P)).then_inc(s["d_w"], 16)
            with sp.Fori(1, N_BATCH) as b:
                wait(sp, "d_x", 16 * b)
                sp.dma_start(X[:, ds(TPB * b, TPB), :], x_rows[:, ds(TPB * b, TPB), :]).then_inc(s["d_x"], 16)
                wait(sp, "pe_ctxT", b)
                sp.dma_start(ctx_b[:, :, :], ctx_rows[:, ds(TPB * b, TPB), :]).then_inc(s["d_ctx"], 16)
                wait(sp, "dve_h", TPB * b)
                sp.dma_start(h_rows[:, ds(TPB * b - TPB, TPB), :], HR[:, :, :]).then_inc(s["d_h"], 16)
            wait(sp, "dve_h", NT)
            sp.dma_start(h_rows[:, NT - TPB:NT, :], HR[:, :, :]).then_inc(s["d_h"], 16)

            wu_rows = w_up.rearrange("e (h p) n -> p (e h) n", p=P)
            wd_rows = w_down.rearrange("e (k p) n -> p (e k) n", p=P)

            def load(e, slot):
                sp.dma_start(wu[:, slot, :, :], wu_rows[:, ds(e * HB, HB), :]).then_inc(d_wt[slot], 16)
                sp.dma_start(wd[:, slot, :, :], wd_rows[:, ds(e * IB, IB), :]).then_inc(d_wt[slot], 16)

            for e in range(W_SLOTS):
                load(e, e)
            for e in range(W_SLOTS - 1):
                sp.wait_ge(d_wt[e], 32)
                sp.sem_inc(s["sp_w"], 1)
            wait(sp, "dve_tab", 2)
            with sp.Fori(W_SLOTS, E - W_SLOTS + 1, W_SLOTS) as i:
                for j in range(W_SLOTS):
                    free_at = sp.value_load(done_tab[0:1, ds(i + (j - W_SLOTS), 1)], min_val=1, max_val=N_TILES + 1)
                    wait(sp, "pe_ed", free_at)
                    load(i + j, j)
                    before = (j - 1) % W_SLOTS
                    sp.wait_ge(d_wt[before], 8 * (i + (j - 1 - before)) + 32)
                    sp.sem_inc(s["sp_w"], 1)
            sp.wait_ge(d_wt[W_SLOTS - 1], 32 * (E // W_SLOTS))
            sp.sem_inc(s["sp_w"], 1)

            out_rows = out.rearrange("b (t p) n -> p (b t) n", p=P)
            with sp.Fori(0, NT) as t:
                wait(sp, "dve_out", t + 1)
                sp.dma_start(out_rows[:, ds(t, 1), :], X[:, ds(t, 1), :]).then_inc(s["d_out"], 16)
            wait(sp, "d_out", 16 * NT)

        @blk.gpsimd
        def _(pool):
            c = s["pool_c"]
            pool.memset(ident[:, :], 0.0).then_inc(c, 1)
            pool.memset(lower[:, :], 0.0).then_inc(c, 1)
            pool.memset(ones[:, :], 1.0).then_inc(c, 1)
            pool.memset(zeros[:, :], 0.0).then_inc(c, 1)
            pool.memset(mhalf[:, :], -0.5).then_inc(c, 1)
            pool.memset(lt44[:, :, :], 0.0).then_inc(c, 1)
            pool.memset(onesE[:, :], 1.0).then_inc(c, 1)
            pool.iota(iota_i[:, :], pattern=[[1, P]], base=0, channel_multiplier=0).then_inc(c, 1)
            pool.iota(part_i[:, :], pattern=[[0, 1]], base=0, channel_multiplier=1).then_inc(c, 1)
            pool.iota(tok_i[:, :], pattern=[[P, NT]], base=0, channel_multiplier=1).then_inc(c, 1)
            wait(pool, "pool_c", 10)
            pool.affine_select(out=ident[:, :], in_=ident[:, :], compare_op=ALU.not_equal, fill=1.0,
                               base=0, pattern=[[-1, P]], channel_multiplier=1).then_inc(c, 1)
            pool.affine_select(out=lower[:, :], in_=lower[:, :], compare_op=ALU.is_ge, fill=1.0,
                               base=0, pattern=[[-1, P]], channel_multiplier=1).then_inc(c, 1)
            pool.affine_select(out=lt44[:, :, :], in_=lt44[:, :, :], compare_op=ALU.is_ge, fill=1.0,
                               base=0, pattern=[[-1, GROUPS], [1, GROUPS]], channel_multiplier=0).then_inc(c, 1)
            pool.tensor_copy(iota_f[:, :], iota_i[:, :]).then_inc(c, 1)
            pool.tensor_copy(iota_h[:, :], iota_i[:, :]).then_inc(c, 1)
            pool.tensor_copy(part_f[:, :], part_i[:, :]).then_inc(c, 1)
            pool.tensor_copy(tok_f[:, :], tok_i[:, :]).then_inc(c, 1)
            pool.tensor_scalar(edge[:, :], iota_i[:, 0:NT], float(P), 0.0, ALU.mult, ALU.add).then_inc(c, 1)

            with pool.Fori(0, N_BATCH) as b:
                for j in range(3):
                    wait(pool, "dve_v", 3 * b + j + 1)
                    pool.tensor_tensor(rstd[:, j, :], veps[:, :], mhalf[:, :], ALU.pow).then_inc(s["pool_r"], 1)

            wait(pool, "dve_idx", 1)
            wait(pool, "d_h", 16 * N_BATCH)

            def gather(i, u, first):
                if not first:
                    wait_first(pool, "pe_xT", i + (u - UNROLL + 1))
                pool.tensor_copy(idx_now[:, u:u + 1], idx_g[:, ds(i + u, 1)]).then_inc(s["pool_idx"], 1)
                gate_pool(pool, "pool_idx", i + u + 1)
                pool.indirect_dma_start(out=xg[:, u, :], out_offset=None, in_=h_dram[:, :],
                                        in_offset=bass.IndirectOffsetOnAxis(ap=idx_now[:, u:u + 1], axis=0),
                                        bounds_check=NT * P - 1).then_inc(d_xg[u], 16)

            for u in range(UNROLL):
                gather(0, u, True)
            with pool.Fori(UNROLL, N_TILES - UNROLL + 1, UNROLL) as i:
                for u in range(UNROLL):
                    gather(i, u, False)

            for u in range(UNROLL):
                pool.wait_ge(d_y[u], 16 * (N_TILES // UNROLL))

            def combine(t, u, first):
                if not first:
                    wait_first(pool, "dve_cmb", TOPK * (t + (u - 1)))
                pool.tensor_copy(yidx[:, u, :], s4i[:, ds((t + u) * TOPK, TOPK)]).then_inc(s["pool_cidx"], 1)
                gate_pool(pool, "pool_cidx", t + u + 1)
                for k in range(TOPK):
                    pool.indirect_dma_start(out=yg[:, u, k, :], out_offset=None, in_=y_dram[:, :],
                                            in_offset=bass.IndirectOffsetOnAxis(ap=yidx[:, u, k:k + 1], axis=0),
                                            bounds_check=N_TILES * P - 1).then_inc(d_yg[u], 16)

            for u in range(2):
                combine(0, u, True)
            with pool.Fori(2, NT - 1, 2) as t:
                for u in range(2):
                    combine(t, u, False)

        @blk.scalar
        def _(ac):
            def go(out_, in_, func, name, **kw):
                return ac.activation(out_, in_, func, **kw).then_inc(s[name], 1)

            wait(ac, "d_small", 16 * 8)
            go(g_tanh[:, :], g_raw[:, :], ACT.Tanh, "act_c")
            wait(ac, "pe_wk", 1)
            go(wkT[:, :], T[0][:, 0:DC], ACT.Copy, "act_c")

            def attend(b):
                wait(ac, "pe_ctxT", b + 1)
                go(ctxT[:, :], T[0][:, :], ACT.Copy, "act_ctxT")
                wait(ac, "pe_kvT", b + 1)
                go(kvT[:, :], U[0][:, :], ACT.Identity, "act_kvT", bias=bk[:, 0:1])
                for jb in (0, 2):
                    wait(ac, "pe_pT", TPB * b + jb + 1)
                    go(pT[:, jb, :], T[0][:, :], ACT.Copy, "act_pT")
                wait(ac, "pe_outT", b + 1)
                go(outT[:, :], U[1][:, :], ACT.Copy, "act_outT", scale=float(SEQ) ** -0.5)
                for it in range(TPB):
                    wait(ac, "pe_sim", TPB * b + it + 1)
                    go(PS[:, it, :], D[it][:, :], ACT.Copy, "act_sim")

            def relu(b, k):
                wait(ac, "pe_up", SB * b + k + 1)
                if k >= 2:
                    wait(ac, "dve_act", SB * b + k - 1)
                elif not (isinstance(b, int) and b == 0):
                    wait(ac, "dve_act", SB * b)
                go(rel[:, k % 2, :], U[k % 2][:, :], ACT.Relu, "act_r")

            def exps(b, it):
                wait(ac, "dve_z", TPB * b + it + 1)
                if it >= 2:
                    wait(ac, "dve_x1", TPB * b + it - 1)
                elif not (isinstance(b, int) and b == 0):
                    wait(ac, "dve_x1", TPB * b + it - 1)
                go(ex[:, it % 2, :], t2[:, it % 2, :], ACT.Exp, "act_e",
                   bias=nmax[:, it:it + 1], accum_out=esum[:, it:it + 1])

            def ends(b):
                slot = b % 2
                for it in (0, 2):
                    wait(ac, "pe_hT", TPB * b + it + 1)
                    dst = hT2[:, ds(slot * (HB * SEQ), HB * SEQ)].rearrange("p (h n) -> p h n", h=HB)
                    go(dst[:, :, it * P:(it + 1) * P], T[0][:, :].rearrange("p (h n) -> p h n", h=HB),
                       ACT.Copy, "act_hT")
                wait(ac, "pe_lgT", b + 1)
                go(lgT[:, :], U[0][0:E, :], ACT.Copy, "act_lgT")

            attend(0)
            for it in range(TPB):
                exps(0, it)
            ends(0)
            with ac.Fori(1, N_BATCH) as b:
                attend(b)
                for it in range(TPB):
                    exps(b, it)
                    relu(b - 1, 2 * it)
                    relu(b - 1, 2 * it + 1)
                ends(b)
            wait(ac, "dve_lg", N_BATCH)
            go(sc[:, :, :], LG[:, :, :], ACT.Sigmoid, "act_sc")
            for k in range(SB):
                relu(N_BATCH - 1, k)

            def tile_in(i, u):
                wait(ac, "pe_xT", i + u + 1)
                go(xgT[:, u % 2, :, :], T[u % 2][:, :].rearrange("p (h n) -> p h n", h=HB), ACT.Copy, "act_xT")

            def tile_relu(i, u):
                wait(ac, "pe_eu", i + u + 1)
                go(erel[:, u % 2, :], U[u % 2][:, 0:INNER], ACT.Relu, "act_er")

            def store(i, u):
                wait(ac, "dve_y", i + u + 1)
                ac.dma_start(y_dram[ds((i + u) * P, P), :], yb[:, u, :]).then_inc(d_y[u], 16)

            tile_in(0, 0)
            tile_relu(0, 0)
            tile_in(0, 1)
            with ac.Fori(0, N_TILES - 2 * UNROLL + 1, UNROLL) as i:
                for u in range(UNROLL):
                    tile_in(i, u + 2)
                    tile_relu(i, u + 1)
                    store(i, u)
            for u in range(UNROLL):
                if u + 2 < UNROLL:
                    tile_in(N_TILES - UNROLL, u + 2)
                if u + 1 < UNROLL:
                    tile_relu(N_TILES - UNROLL, u + 1)
                store(N_TILES - UNROLL, u)

        @blk.vector
        def _(ve):
            chain = [0]

            def link(ins):
                chain[0] += 1
                ins.then_inc(s["dve_ch"], 1)
                wait(ve, "dve_ch", chain[0])

            ve.memset(pre[:, 0, :], 0.0).then_inc(s["dve_sh"], 1)
            wait(ve, "d_small", 16 * 8)
            wait(ve, "act_c", 1)

            STEPS = 40

            def batch(b, shared):
                first = isinstance(b, int) and b == 0
                n = [0]

                def step(ins):
                    n[0] += 1
                    ins.then_inc(s["dve_e"], 1)

                def settle(w=wait):
                    w(ve, "dve_e", STEPS * b + n[0])

                def Xt(it):
                    return X2[:, ds((TPB * b + it) * H, H)]

                def stats(src, eps, which):
                    for it in range(TPB):
                        step(ve.bn_stats(bst[:, it, :], src(it)))
                    settle()
                    ve.memset(gate_v[:, :], 0.0)
                    for it in range(TPB):
                        step(ve.bn_aggr(mv[:, it, :], bst[:, it, :]))
                    settle()
                    ve.tensor_scalar(veps[:, :], mv[:, :, 1], eps, None, ALU.add).then_inc(s["dve_v"], 1)
                    wait(ve, "pool_r", 3 * b + which + 1)

                wait_first(ve, "d_x", 16 * b + 16)
                stats(Xt, 1e-5, 0)
                for it in range(TPB):
                    ve.tensor_scalar(PS[:, it, :], Xt(it), mv[:, it, 0:1], rstd[:, 0, it:it + 1],
                                     ALU.subtract, ALU.mult).then_inc(s["dve_p"], 1)
                wait(ve, "pe_kv", b + 1)
                ve.tensor_copy(kv[:, :, :], T[1][:, :].rearrange("p (j d) -> p j d", d=DC)).then_inc(s["dve_kv"], 1)
                for jb in (1, 3):
                    wait(ve, "pe_pT", TPB * b + jb + 1)
                    ve.tensor_copy(pT[:, jb, :], T[1][:, :]).then_inc(s["dve_pT"], 1)
                wait_first(ve, "act_sim", TPB * b + TPB)
                stats(lambda it: PS[:, it, :], 1e-6, 1)
                for it in range(TPB):
                    step(ve.scalar_tensor_tensor(t1[:, it % 2, :], PS[:, it, :], mv[:, it, 0:1], gam[:, :],
                                                 ALU.subtract, ALU.mult))
                    settle()
                    if it >= 2:
                        wait(ve, "act_e", TPB * b + it - 1)
                    elif not first:
                        wait(ve, "act_e", TPB * b)
                    step(ve.scalar_tensor_tensor(t2[:, it % 2, :], t1[:, it % 2, :], rstd[:, 1, it:it + 1],
                                                 bet[:, :], ALU.mult, ALU.add))
                    settle()
                    ve.tensor_reduce(nmax[:, it:it + 1], t2[:, it % 2, :], AX.X, ALU.max,
                                     negate=True).then_inc(s["dve_z"], 1)
                    if shared:
                        square(b - 1, 2 * it)
                        square(b - 1, 2 * it + 1)
                    wait(ve, "act_e", TPB * b + it + 1)
                    step(ve.reciprocal(esum[:, it:it + 1], esum[:, it:it + 1]))
                    settle()
                    step(ve.tensor_tensor(ecoef[:, it:it + 1], esum[:, it:it + 1], g_tanh[:, 0:1], ALU.mult))
                    settle()
                    ve.scalar_tensor_tensor(Xt(it), ex[:, it % 2, :], ecoef[:, it:it + 1], Xt(it),
                                            ALU.mult, ALU.add).then_inc(s["dve_x1"], 1)
                wait_first(ve, "dve_x1", TPB * b + TPB)
                stats(Xt, 1e-5, 2)
                if not first:
                    wait(ve, "d_h", 16 * b)
                for it in range(TPB):
                    ve.tensor_scalar(HR[:, it, :], Xt(it), mv[:, it, 0:1], rstd[:, 2, it:it + 1],
                                     ALU.subtract, ALU.mult).then_inc(s["dve_h"], 1)
                if shared:
                    add_shared(b - 1)
                slot = b % 2
                for it in (1, 3):
                    wait(ve, "pe_hT", TPB * b + it + 1)
                    dst = hT2[:, ds(slot * (HB * SEQ), HB * SEQ)].rearrange("p (h n) -> p h n", h=HB)
                    ve.tensor_copy(dst[:, :, it * P:(it + 1) * P],
                                   T[1][:, :].rearrange("p (h n) -> p h n", h=HB)).then_inc(s["dve_hT"], 1)
                wait(ve, "pe_lg", b + 1)
                ve.tensor_copy(LG2[:, ds(b * (TPB * E), TPB * E)], U[1][:, 0:TPB * E]).then_inc(s["dve_lg"], 1)
                wait(ve, "dve_h", TPB * b + TPB)
                assert n[0] == STEPS, n

            def square(b, k):
                wait(ve, "act_r", SB * b + k + 1)
                if k >= 2:
                    wait(ve, "pe_down", SB * b + k - 1)
                elif not (isinstance(b, int) and b == 0):
                    wait(ve, "pe_down", SB * b)
                ve.scalar_tensor_tensor(act[:, k % 2, :], U[k % 2][:, :], 0.0, rel[:, k % 2, :],
                                        ALU.max, ALU.mult).then_inc(s["dve_act"], 1)

            def add_shared(b):
                wait(ve, "pe_down", SB * b + SB)
                for it in range(TPB):
                    xs = X2[:, ds((TPB * b + it) * H, H)]
                    ve.scalar_tensor_tensor(xs, D[it][:, :], g_tanh[:, 1:2], xs, ALU.mult, ALU.add)\
                      .then_inc(s["dve_sh"], 1)

            batch(0, False)
            with ve.Fori(1, N_BATCH) as b:
                batch(b, True)

            last = N_BATCH - 1
            wait(ve, "act_sc", 1)
            wait(ve, "pool_c", 18)
            grp = lambda t: t[:, :, :].rearrange("p t (g e) -> p (t g) e", e=EG)
            m1, cnt, m2, q, gs, gm = (gsm[:, j, :] for j in range(6))
            bc8 = lambda a: a.unsqueeze(2).broadcast_to([P, NT * GROUPS, EG])
            link(ve.tensor_tensor(sfc[:, :, :], sc[:, :, :], ebias[:, :].unsqueeze(1).broadcast_to([P, NT, E]), ALU.add))
            link(ve.tensor_reduce(m1, grp(sfc), AX.X, ALU.max))
            link(ve.tensor_tensor(grp(sm), grp(sfc), bc8(m1), ALU.is_equal))
            link(ve.tensor_reduce(cnt, grp(sm), AX.X, ALU.add))
            square(last, 0)
            link(ve.scalar_tensor_tensor(sm[:, :, :], sm[:, :, :], FAR, sfc[:, :, :], ALU.mult, ALU.add))
            link(ve.tensor_reduce(m2, grp(sm), AX.X, ALU.max))
            link(ve.tensor_scalar(q, cnt, 2.0, FAR, ALU.is_lt, ALU.mult))
            link(ve.tensor_tensor(q, q, m1, ALU.add))
            link(ve.tensor_tensor(m2, m2, q, ALU.max))
            link(ve.tensor_tensor(gs, m1, m2, ALU.add))
            g3 = gs.rearrange("p (t g) -> p t g", g=GROUPS)
            other = g3.unsqueeze(2).broadcast_to([P, NT, GROUPS, GROUPS])
            own = g3.unsqueeze(3).broadcast_to([P, NT, GROUPS, GROUPS])
            link(ve.tensor_tensor(gcmp[:, 0, :, :, :], other, own, ALU.is_gt))
            link(ve.tensor_tensor(gcmp[:, 1, :, :, :], other, own, ALU.is_equal))
            square(last, 1)
            link(ve.tensor_tensor(gcmp[:, 1, :, :, :], gcmp[:, 1, :, :, :],
                                  lt44[:, :, :].unsqueeze(1).broadcast_to([P, NT, GROUPS, GROUPS]), ALU.mult))
            link(ve.tensor_tensor(gcmp[:, 0, :, :, :], gcmp[:, 0, :, :, :], gcmp[:, 1, :, :, :], ALU.add))
            link(ve.tensor_reduce(gm, gcmp[:, 0, :, :, :].rearrange("p t g h -> p (t g) h"), AX.X, ALU.add))
            link(ve.tensor_scalar(gm, gm, float(TOP_GROUPS), None, ALU.is_lt))
            link(ve.tensor_tensor(grp(sm), grp(sfc), bc8(gm), ALU.mult))
            for t in range(NT):
                ve.max(top8[:, t, :], sm[:, t, :]).then_inc(s["dve_ch"], 1)
            chain[0] += NT
            wait(ve, "dve_ch", chain[0])
            for t in range(NT):
                ve.max_index(idx8[:, t, :], top8[:, t, :], sm[:, t, :]).then_inc(s["dve_ch"], 1)
            chain[0] += NT
            wait(ve, "dve_ch", chain[0])
            square(last, 2)
            link(ve.tensor_copy(idxf[:, :, :], idx8[:, :, 0:TOPK]))
            o3 = oneh[:, :, :, :].rearrange("p t k e -> p (t k) e")
            t3 = tmp[:, :, :, :].rearrange("p t k e -> p (t k) e")
            link(ve.tensor_tensor(o3, iota_f[:, 0:E].unsqueeze(1).broadcast_to([P, NT * TOPK, E]),
                                  idxf[:, :, :].rearrange("p t k -> p (t k)").unsqueeze(2)
                                  .broadcast_to([P, NT * TOPK, E]), ALU.is_equal))
            with nc.allow_low_precision("sums are 0 or 1"):
                ve.tensor_reduce(chosen[:, :, :], oneh[:, :, :, :].rearrange("p t k e -> p t e k"), AX.X, ALU.add)\
                  .then_inc(s["dve_M"], 1)
            square(last, 3)
            byk = lambda t: t.unsqueeze(2).broadcast_to([P, NT, TOPK, E])
            link(ve.tensor_tensor(tmp[:, :, :, :], oneh[:, :, :, :], byk(sc[:, :, :]), ALU.mult))
            link(ve.tensor_reduce(w4[:, :], t3, AX.X, ALU.add))
            w3 = w4[:, :].rearrange("p (t k) -> p t k", k=TOPK)
            link(ve.tensor_reduce(wsum[:, :], w3, AX.X, ALU.add))
            link(ve.tensor_scalar(wsum[:, :], wsum[:, :], 1e-20, None, ALU.add))
            link(ve.reciprocal(wsum[:, :], wsum[:, :]))
            link(ve.tensor_tensor(w3, w3, wsum[:, :].unsqueeze(2).broadcast_to([P, NT, TOPK]), ALU.mult))
            link(ve.tensor_scalar(w4[:, :], w4[:, :], SCALE, g_tanh[:, 1:2], ALU.mult, ALU.mult))
            square(last, 4)
            wait(ve, "pe_rank", 1)
            for t in range(NT):
                link(ve.tensor_tensor(pre[:, t + 1, :], pre[:, t, :], T[1][:, t * E:(t + 1) * E], ALU.add))
            square(last, 5)
            c3 = tmp[:, 0:NT // TOPK, :, :].rearrange("p t k e -> p (t k e)").rearrange("p (e j) -> p e j", e=E)
            link(ve.tensor_tensor(c3, pre[:, NT, :].unsqueeze(2).broadcast_to([P, E, NT]),
                                  edge[:, :].unsqueeze(1).broadcast_to([P, E, NT]), ALU.is_gt))
            link(ve.tensor_reduce(n_tl[:, :], c3, AX.X, ALU.add))
            link(ve.tensor_tensor_scan(tend[:, :], onesE[:, :], n_tl[:, :], 0.0, ALU.mult, ALU.add))
            ve.tensor_scalar(done_tab[0:1, :], tend[0:1, :], 1.0, None, ALU.add).then_inc(s["dve_tab"], 1)
            link(ve.tensor_tensor(base[:, :], tend[:, :], n_tl[:, :], ALU.subtract))
            link(ve.tensor_scalar(base[:, :], base[:, :], float(P), None, ALU.mult))
            p16 = pre[:, 0:NT, :]
            link(ve.tensor_tensor(p16, T[0][:, :].rearrange("p (t e) -> p t e", e=E), p16, ALU.add))
            link(ve.tensor_tensor(p16, p16, base[:, :].unsqueeze(1).broadcast_to([P, NT, E]), ALU.add))
            link(ve.tensor_scalar(onesE[:, :], tend[:, :], part_f[:, 0:1], None, ALU.is_le, ALU.add,
                                  accum_out=eid[:, 0:1]))
            link(ve.tensor_scalar(eid[:, 0:1], eid[:, 0:1], float(E - 1), None, ALU.min))
            link(ve.tensor_copy(eid_i[:, 0:1], eid[:, 0:1]))
            link(ve.tensor_scalar(eid_i[:, 1:2], eid_i[:, 0:1], W_SLOTS - 1, None, ALU.bitwise_and))
            link(ve.tensor_copy(eid[:, 1:2], eid_i[:, 1:2]))
            ve.tensor_scalar(eid[:, 0:1], eid[:, 0:1], 1.0, None, ALU.add).then_inc(s["dve_tabT"], 1)
            square(last, 6)
            link(ve.tensor_tensor(tmp[:, :, :, :], oneh[:, :, :, :], byk(p16), ALU.mult))
            link(ve.tensor_reduce(s4[:, :], t3, AX.X, ALU.add))
            link(ve.tensor_copy(s4i[:, :], s4[:, :]))
            link(ve.tensor_scalar(sp_i[:, 0, :], s4i[:, :], P - 1, None, ALU.bitwise_and))
            link(ve.tensor_scalar(sp_i[:, 1, :], s4i[:, :], 7, None, ALU.logical_shift_right))
            link(ve.tensor_copy(sp_f[:, :, :], sp_i[:, :, :]))
            square(last, 7)
            spf2 = sp_f[:, :, :].rearrange("p a n -> p (a n)")
            with ve.Fori(0, NT - 1, 2) as t:
                for u in range(2):
                    wait(ve, "pe_sel", t + u + 1)
                    for k in range(TOPK):
                        at = (t + u) * TOPK + k
                        ve.tensor_scalar(selA[:, u, k, :], iota_h[:, :], spf2[:, ds(at, 1)], None, ALU.is_equal)\
                          .then_inc(s["dve_sel"], 1)
                        ve.tensor_scalar(selB[:, u, k, :], iota_h[:, 0:N_TILES], spf2[:, ds(at + NT * TOPK, 1)],
                                         tok_f[:, ds(t + u, 1)], ALU.is_equal, ALU.mult)\
                          .then_inc(s["dve_sel"], 1)
            wait(ve, "pe_tab", 1)
            ve.tensor_copy(tab[0:1, :], U[1][0:1, 0:2 * P]).then_inc(s["dve_tab"], 1)
            wait(ve, "pe_ix", 1)
            ve.tensor_copy(idx_g[:, :], T[0][:, 0:N_TILES]).then_inc(s["dve_idx"], 1)
            add_shared(last)
            wait(ve, "dve_sh", 1 + NT)

            def tile_square(i, u):
                wait(ve, "act_er", i + u + 1)
                ve.scalar_tensor_tensor(eact[:, u % 2, :], U[u % 2][:, 0:INNER], 0.0, erel[:, u % 2, :],
                                        ALU.max, ALU.mult).then_inc(s["dve_eact"], 1)

            def tile_actT(i, u):
                wait(ve, "pe_eT", i + u + 1)
                ve.tensor_copy(eactT[:, u % 2, :, :],
                               D[u % 2][:, 0:INNER].rearrange("p (k n) -> p k n", k=IB)).then_inc(s["dve_eT"], 1)

            def tile_out(i, u, first):
                wait(ve, "pe_ed", i + u + 2)
                if not first:
                    ve.wait_ge(d_y[u], 4 * i)
                ve.tensor_copy(yb[:, u, :], D[2 + u % 2][:, :]).then_inc(s["dve_y"], 1)

            tile_square(0, 0)

            def tiles(i, first=False, final=False):
                for u in range(UNROLL):
                    tile_actT(i, u)
                    if not (final and u == UNROLL - 1):
                        tile_square(i, u + 1)
                    tile_out(i, u, first)

            tiles(0, first=True)
            with ve.Fori(UNROLL, N_TILES - 2 * UNROLL + 1, UNROLL) as i:
                tiles(i)
            tiles(N_TILES - UNROLL, final=True)

            with ve.Fori(0, NT - 1, 2) as t:
                for u in range(2):
                    ve.wait_ge(d_yg[u], 8 * TOPK * t + 16 * TOPK)
                    xs = X2[:, ds((t + u) * H, H)]
                    for k in range(TOPK):
                        w = w4[:, ds((t + u) * TOPK + k, 1)]
                        if k:
                            wait(ve, "dve_cmb", TOPK * (t + u) + k)
                        ve.scalar_tensor_tensor(xs, yg[:, u, k, :], w, xs, ALU.mult, ALU.add)\
                          .then_inc(s["dve_cmb"], 1)
                    wait(ve, "dve_cmb", TOPK * (t + u) + TOPK)
                    ve.sem_inc(s["dve_out"], 1)

        @blk.tensor
        def _(pe):
            def mm(o, l, r, start=True, stop=True):
                return pe.matmul(o, l, r, start=start, stop=stop)

            wait(pe, "d_small", 16 * 8)
            wait(pe, "pool_c", 18)
            pe.transpose(T[0][:, 0:DC], wk[:, :], ident[:, :]).then_inc(s["pe_wk"], 1)
            wait(pe, "act_c", 2)

            def attend(b):
                first = isinstance(b, int) and b == 0
                wait(pe, "d_ctx", 16 * b + 16)
                if not first:
                    wait(pe, "act_hT", 2 * b)
                for j in range(TPB):
                    i_ = pe.transpose(T[0][:, j * P:(j + 1) * P], ctx_b[:, j, :], ident[:, :])
                i_.then_inc(s["pe_ctxT"], 1)
                wait(pe, "act_ctxT", b + 1)
                if not first:
                    wait(pe, "act_lgT", b)
                mm(U[0][:, :], wkT[:, :], ctxT[:, :]).then_inc(s["pe_kvT"], 1)
                wait(pe, "act_kvT", b + 1)
                if not first:
                    wait(pe, "dve_hT", 2 * b)
                for j in range(TPB):
                    i_ = pe.transpose(T[1][:, j * P:(j + 1) * P], kvT[:, j * P:(j + 1) * P], ident[:, :])
                i_.then_inc(s["pe_kv"], 1)
                wait(pe, "dve_p", TPB * b + TPB)

                def p_block(j):
                    for it in range(TPB):
                        i_ = pe.transpose(T[j % 2][:, it * P:(it + 1) * P], PS[:, it, j * P:(j + 1) * P], ident[:, :])
                    i_.then_inc(s["pe_pT"], 1)

                def o_block(j):
                    return mm(U[1][:, :], kv[:, j, :], pT[:, j, :], j == 0, j == TPB - 1)

                p_block(0)
                wait(pe, "dve_kv", b + 1)
                p_block(1)
                wait(pe, "act_pT", 2 * b + 1)
                p_block(2)
                if not first:
                    wait(pe, "dve_lg", b)
                o_block(0)
                wait(pe, "dve_pT", 2 * b + 1)
                p_block(3)
                o_block(1)
                wait(pe, "act_pT", 2 * b + 2)
                o_block(2)
                wait(pe, "dve_pT", 2 * b + 2)
                o_block(3).then_inc(s["pe_outT"], 1)
                wait(pe, "act_outT", b + 1)
                if not first:
                    wait(pe, "dve_sh", TPB * b - TPB + 1)
                for it in range(TPB):
                    mm(D[it][:, :], outT[:, it * P:(it + 1) * P], kvT[:, :]).then_inc(s["pe_sim"], 1)

            def shared_up(b, k):
                if k >= 2:
                    wait(pe, "dve_act", SB * b + k - 1)
                slot = b % 2
                for h in range(HB):
                    i_ = mm(U[k % 2][:, :], wsu[:, h, k * P:(k + 1) * P],
                            hT2[:, ds((slot * HB + h) * SEQ, SEQ)], h == 0, h == HB - 1)
                i_.then_inc(s["pe_up"], 1)

            def shared_down(b, k):
                wait(pe, "dve_act", SB * b + k + 1)
                for it in range(TPB):
                    i_ = mm(D[it][:, :], act[:, k % 2, it * P:(it + 1) * P], wsd[:, k, :], k == 0, k == SB - 1)
                i_.then_inc(s["pe_down"], 1)

            def shared(b, ks):
                for k in ks:
                    if k == 0:
                        shared_up(b, 0)
                    if k + 1 < SB:
                        shared_up(b, k + 1)
                    shared_down(b, k)

            def ends(b):
                first = isinstance(b, int) and b == 0
                for it in range(TPB):
                    wait(pe, "dve_h", TPB * b + it + 1)
                    if it < 2:
                        wait(pe, ("act_pT", "dve_pT")[it], 2 * b + 2)
                    else:
                        wait(pe, ("act_hT", "dve_hT")[it - 2], 2 * b + 1)
                    for h in range(HB):
                        i_ = pe.transpose(T[it % 2][:, h * P:(h + 1) * P], HR[:, it, h * P:(h + 1) * P], ident[:, :])
                    i_.then_inc(s["pe_hT"], 1)
                wait(pe, "act_hT", 2 * b + 2)
                wait(pe, "dve_hT", 2 * b + 2)
                if not first:
                    wait(pe, "dve_act", SB * b)
                slot = b % 2
                for h in range(HB):
                    i_ = mm(U[0][0:E, :], gate[:, h, :], hT2[:, ds((slot * HB + h) * SEQ, SEQ)], h == 0, h == HB - 1)
                i_.then_inc(s["pe_lgT"], 1)
                wait_first(pe, "act_lgT", b + 1)
                for it in range(TPB):
                    i_ = pe.transpose(U[1][:, it * E:(it + 1) * E], lgT[:, it * P:(it + 1) * P], ident[0:E, 0:E])
                i_.then_inc(s["pe_lg"], 1)

            attend(0)
            ends(0)
            wait(pe, "d_w", 32)
            with pe.Fori(1, N_BATCH) as b:
                attend(b)
                wait(pe, "act_sim", TPB * b + TPB)
                shared(b - 1, range(SB))
                ends(b)
            last = N_BATCH - 1
            wait(pe, "dve_lg", N_BATCH)
            wait(pe, "dve_sh", 1 + TPB * last)
            shared(last, range(0, 4))
            wait(pe, "dve_M", 1)
            ch = chosen[:, :, :].rearrange("p t e -> p (t e)")
            mm(T[0][:, :], lower[:, :], ch)
            mm(T[1][:, :], ones[:, :], ch).then_inc(s["pe_rank"], 1)
            shared(last, range(4, SB))
            wait(pe, "dve_act", SB * N_BATCH)
            wait(pe, "dve_tabT", 1)
            for j in range(2):
                i_ = pe.transpose(U[1][0:1, j * P:(j + 1) * P], eid[:, j:j + 1], ident[:, :])
            i_.then_inc(s["pe_tab"], 1)
            pe.sem_inc(s["pe_sel"], 2)
            wait(pe, "dve_sel", 2 * TOPK)
            mm(T[0][:, 0:N_TILES], zeros[:, :], zeros[:, 0:N_TILES], True, False)
            with pe.Fori(0, NT - 1, 2) as t:
                for u in range(2):
                    wait(pe, "dve_sel", 2 * TOPK * (t + u + 1))
                    for k in range(TOPK):
                        i_ = mm(T[0][:, 0:N_TILES], selA[:, u, k, :], selB[:, u, k, :], False, False)
                    i_.then_inc(s["pe_sel"], 1)
            mm(T[0][:, 0:N_TILES], zeros[:, :], zeros[:, 0:N_TILES], False, True).then_inc(s["pe_ix"], 1)

            wait(pe, "dve_tab", 2)

            def rows(i, u, first):
                pe.wait_ge(d_xg[u % UNROLL], 4 * (i + (u - u % UNROLL)) + 16)
                if not first:
                    wait(pe, "act_xT", i + (u - 1))
                for h in range(HB):
                    i_ = pe.transpose(T[u % 2][:, h * P:(h + 1) * P], xg[:, u % UNROLL, h * P:(h + 1) * P], ident[:, :])
                i_.then_inc(s["pe_xT"], 1)

            slots = [pe.alloc_register(f"w_slot{j}") for j in range(2)]

            def up(i, u, first):
                ready = pe.value_load(tab[0:1, ds(i + u, 1)], min_val=1, max_val=E)
                slot = pe.value_load(tab[0:1, ds(i + (u + P), 1)], min_val=0, max_val=W_SLOTS - 1)
                wait(pe, "sp_w", ready)
                wait(pe, "act_xT", i + (u + 1))
                if not first:
                    wait(pe, "dve_eact", i + (u - 1))
                for h in range(HB):
                    i_ = mm(U[u % 2][:, 0:INNER], xgT[:, u % 2, h, :],
                            wu2[:, ds((slot * HB + h) * INNER, INNER)], h == 0, h == HB - 1)
                i_.then_inc(s["pe_eu"], 1)
                return slot

            def act_t(i, u, first):
                wait(pe, "dve_eact", i + (u + 1))
                if not first:
                    wait(pe, "dve_eT", i + (u - 1))
                for k in range(IB):
                    i_ = pe.transpose(D[u % 2][:, k * P:(k + 1) * P], eact[:, u % 2, k * P:(k + 1) * P], ident[:, :])
                i_.then_inc(s["pe_eT"], 1)

            def down(i, u, first):
                slot = pe.value_load(tab[0:1, ds(i + (u + P), 1)], min_val=0, max_val=W_SLOTS - 1)
                wait(pe, "dve_eT", i + (u + 1))
                if not first:
                    wait(pe, "dve_y", i + (u - 1))
                for k in range(IB):
                    i_ = mm(D[2 + u % 2][:, :], eactT[:, u % 2, k, :],
                            wd2[:, ds((slot * IB + k) * H, H)], k == 0, k == IB - 1)
                i_.then_inc(s["pe_ed"], 1)

            pe.sem_inc(s["pe_ed"], 1)
            rows(0, 0, True)
            up(0, 0, True)
            rows(0, 1, True)

            def tiles(i, first=False, final=False):
                for u in range(UNROLL):
                    act_t(i, u, first and u < 2)
                    if not (final and u + 2 >= UNROLL):
                        rows(i, u + 2, False)
                    if not (final and u + 1 >= UNROLL):
                        up(i, u + 1, first and u + 1 < 2)
                    down(i, u, first and u < 2)

            tiles(0, first=True)
            with pe.Fori(UNROLL, N_TILES - 2 * UNROLL + 1, UNROLL) as i:
                tiles(i)
            tiles(N_TILES - UNROLL, final=True)


_INS = ["x", "ctx_512", "g_xattn", "g_ffn", "L0_xattn_W_k", "L0_xattn_b_k", "L0_xattn_ln_gamma",
        "L0_xattn_ln_beta", "L0_ffn_gate_w", "L0_ffn_e_bias", "L0_ffn_Wu", "L0_ffn_Wd", "L0_ffn_Wsu",
        "L0_ffn_Wsd"]


def kernel(**inputs):
    import numpy as np
    import concourse.bacc as bacc
    from concourse.bass_utils import run_bass_kernel_spmd

    nc = bacc.Bacc("TRN2", target_bir_lowering=False, num_devices=1)
    arrays, args = {}, []
    for name in _INS:
        a = np.ascontiguousarray(inputs[name])
        arrays[f"in_{name}"] = a
        args.append(nc.dram_tensor(f"in_{name}", a.shape, mybir.dt.from_np(a.dtype), kind="ExternalInput").ap())
    out = nc.dram_tensor("out", inputs["x"].shape, mybir.dt.float32, kind="ExternalOutput").ap()
    block_kernel(nc, *args, out)
    r = run_bass_kernel_spmd(nc, [arrays], core_ids=[0])
    return r.results[0]["out"]
```

```python
from contextlib import ExitStack

import concourse.bass as bass
from concourse import mybir

P = 128
N_BATCH, SEQ, H = 4, 512, 512
DC = 128
TPB = SEQ // P
NT = N_BATCH * TPB
HB = H // P
E, INNER = 32, 256
IB = INNER // P
SI = 1024
SB = SI // P
TOPK, GROUPS, TOP_GROUPS, SCALE = 4, 4, 2, 2.5
EG = E // GROUPS
UNROLL = 4
N_TILES = -(-((NT * P * TOPK + E * (P - 1)) // P) // UNROLL) * UNROLL
W_SLOTS = 4
FAR = -1.0e30


def block_kernel(nc, x, ctx_in, g_xattn, g_ffn, w_k, b_k, ln_gamma, ln_beta,
                 gate_w, e_bias, w_up, w_down, w_sh_up, w_sh_down, out):
    f32, i32, u32 = mybir.dt.float32, mybir.dt.int32, mybir.dt.uint32
    f16, bf16 = mybir.dt.float16, mybir.dt.bfloat16
    ALU, ACT, AX = mybir.AluOpType, mybir.ActivationFunctionType, mybir.AxisListType
    ds = bass.ds

    with ExitStack() as stack:
        def sb(name, shape, dt=f32):
            return stack.enter_context(nc.sbuf_tensor(name, shape, dt))

        def bank(name):
            return stack.enter_context(nc.psum_tensor(name, [P, 512], f32))

        def sem(name):
            return stack.enter_context(nc.semaphore(name))

        h_dram = nc.dram_tensor("h_rows", (NT * P, H), f32).ap()
        y_dram = nc.dram_tensor("y_rows", (N_TILES * P, H), f32).ap()

        X = sb("X", [P, NT, H])
        X2 = X[:, :, :].rearrange("p t n -> p (t n)")
        HR = sb("HR", [P, TPB, H])
        hT = sb("hT", [P, 2, HB, SEQ])
        hT2 = hT[:, :, :, :].rearrange("p s h n -> p (s h n)")
        wk = sb("wk", [P, DC])
        wkT = sb("wkT", [P, DC])
        bk = sb("bk", [DC, 1])
        g_raw = sb("g_raw", [P, 2])
        g_tanh = sb("g_tanh", [P, 2])
        gate = sb("gate", [P, HB, E])
        ebias = sb("ebias", [P, E])
        wsu = sb("wsu", [P, HB, SI])
        wsd = sb("wsd", [P, SB, H])
        rel = sb("rel", [P, 2, SEQ])
        act = sb("act", [P, 2, SEQ])
        lgT = sb("lgT", [E, SEQ])
        LG = sb("LG", [P, NT, E])
        LG2 = LG[:, :, :].rearrange("p t e -> p (t e)")
        bst = sb("bst", [P, TPB, 6])
        mv = sb("mv", [P, TPB, 2])
        veps = sb("veps", [P, TPB])
        rstd = sb("rstd", [P, 3, TPB])
        nmax = sb("nmax", [P, TPB])
        esum = sb("esum", [P, TPB])
        ecoef = sb("ecoef", [P, TPB])
        ident = sb("ident", [P, P])
        mhalf = sb("mhalf", [P, TPB])
        lower = sb("lower", [P, P], bf16)
        ones = sb("ones", [P, P], bf16)
        zeros = sb("zeros", [P, P], f16)
        iota_i = sb("iota_i", [P, P], i32)
        iota_f = sb("iota_f", [P, P])
        iota_h = sb("iota_h", [P, P], f16)
        part_i = sb("part_i", [P, 1], i32)
        part_f = sb("part_f", [P, 1])
        tok_i = sb("tok_i", [P, NT], i32)
        tok_f = sb("tok_f", [P, NT])
        lt44 = sb("lt44", [P, GROUPS, GROUPS])
        edge = sb("edge", [P, NT])
        sc = sb("sc", [P, NT, E])
        sfc = sb("sfc", [P, NT, E])
        sm = sb("sm", [P, NT, E])
        gsm = sb("gsm", [P, 6, NT * GROUPS])
        gcmp = sb("gcmp", [P, 2, NT, GROUPS, GROUPS])
        top8 = sb("top8", [P, NT, 8])
        idx8 = sb("idx8", [P, NT, 8], u32)
        idxf = sb("idxf", [P, NT, TOPK])
        chosen = sb("chosen", [P, NT, E], bf16)
        w4 = sb("w4", [P, NT * TOPK])
        wsum = sb("wsum", [P, NT])
        pre = sb("pre", [P, NT + 1, E])
        n_tl = sb("n_tl", [P, E])
        tend = sb("tend", [P, E])
        base = sb("base", [P, E])
        onesE = sb("onesE", [P, E])
        s4 = sb("s4", [P, NT * TOPK])
        s4i = sb("s4i", [P, NT * TOPK], u32)
        sp_i = sb("sp_i", [P, 2, NT * TOPK], u32)
        sp_f = sb("sp_f", [P, 2, NT * TOPK])
        eid = sb("eid", [P, 4])
        eid_i = sb("eid_i", [P, 2], i32)
        tab = sb("tab", [1, 2 * P], i32)
        used_tab = sb("used_tab", [1, 2], i32)
        done_tab = sb("done_tab", [1, E], i32)
        selA = sb("selA", [P, 2, TOPK, P], f16)
        selB = sb("selB", [P, 2, TOPK, N_TILES], f16)
        idx_g = sb("idx_g", [P, N_TILES], u32)
        idx_now = sb("idx_now", [P, UNROLL], u32)
        yidx = sb("yidx", [P, UNROLL * TOPK], u32)
        gate_v = sb("gate_v", [P, 1])
        gate_p = sb("gate_p", [1, 2 * UNROLL + 2])
        with ExitStack() as early:
            def at(name, shape, where=early):
                return where.enter_context(nc.sbuf_tensor(name, shape, f32))

            wu = at("wu", [P, W_SLOTS, HB, INNER])
            wd = at("wd", [P, W_SLOTS, IB, H])
            with ExitStack() as attention:
                ctx_b = at("ctx_b", [P, TPB, DC], attention)
                ctxT = at("ctxT", [DC, SEQ], attention)
                kvT = at("kvT", [DC, SEQ], attention)
                kv = at("kv", [P, TPB, DC], attention)
                PS = at("PS", [P, TPB, SEQ], attention)
                pT = at("pT", [P, TPB, SEQ], attention)
                outT = at("outT", [DC, SEQ], attention)
                t1 = at("t1", [P, 2, SEQ], attention)
                t2 = at("t2", [P, 2, SEQ], attention)
                ex = at("ex", [P, 2, SEQ], attention)
                gam = at("gam", [P, SEQ], attention)
                bet = at("bet", [P, SEQ], attention)
            xg = at("xg", [P, UNROLL, H])
            xgT = at("xgT", [P, 2, HB, P])
            erel = at("erel", [P, 2, INNER])
            eact = at("eact", [P, 2, INNER])
            eactT = at("eactT", [P, 2, IB, P])
            yb = at("yb", [P, UNROLL, H])
            tmp = at("tmp", [P, NT, TOPK, E])
            oneh = at("oneh", [P, NT, TOPK, E])
        wu2 = wu[:, :, :, :].rearrange("p s h n -> p (s h n)")
        wd2 = wd[:, :, :, :].rearrange("p s h n -> p (s h n)")
        yg = sb("yg", [P, UNROLL, TOPK, H])

        T = [bank("T0"), bank("T1")]
        U = [bank("U0"), bank("U1")]
        D = [bank("D0"), bank("D1"), bank("D2"), bank("D3")]

        names = """d_fill d_small d_x d_ctx d_w d_h d_out
            pool_c pool_r pool_idx pool_cidx
            dve_v dve_p dve_kv dve_pT dve_z dve_e dve_x1 dve_h dve_act dve_sh dve_hT dve_lg dve_ch
            dve_M dve_slot dve_tab dve_sel dve_cr dve_tabT dve_idx dve_eact dve_eT dve_y dve_out dve_cmb dve_done
            act_c act_ctxT act_kvT act_pT act_outT act_sim act_e act_r act_hT act_lgT act_sc act_xT act_er
            pe_wk pe_ctxT pe_kvT pe_kv pe_pT pe_outT pe_sim pe_up pe_down pe_hT pe_lgT pe_lg pe_rank
            pe_sel pe_tab pe_ix pe_xT pe_eu pe_eT pe_ed
            sp_w""".split()
        s = {n: sem(n) for n in names}
        d_wt = [sem(f"d_wt{i}") for i in range(W_SLOTS)]
        d_xg = [sem(f"d_xg{i}") for i in range(UNROLL)]
        d_y = [sem(f"d_y{i}") for i in range(UNROLL)]
        d_yg = [sem(f"d_yg{i}") for i in range(UNROLL)]

        def wait(eng, name, n):
            eng.wait_ge(s[name], n)

        def wait_first(eng, name, n):
            eng.wait_ge(s["pool_c"], 1)
            eng.wait_ge(s[name], n)

        def load_used(eng):
            wait(eng, "dve_tab", 3)
            return eng.value_load(used_tab[0:1, 0:1], min_val=NT * TOPK, max_val=N_TILES)


        def gate_pool(pool, sem_, n, at=0):
            pool.wait_ge(sem_, n)
            pool.tensor_tensor(gate_p[:, at:at + 1], mhalf[0:1, 0:1], mhalf[0:1, 0:1], ALU.add)

        blk = stack.enter_context(nc.Block())

        @blk.sync
        def _(sp):
            small = [(wk[:, :], w_k), (bk[:, :], b_k.rearrange("(p a) -> p a", a=1)),
                     (gam[:, :], ln_gamma.rearrange("(a n) -> a n", a=1).broadcast_to([P, SEQ])),
                     (bet[:, :], ln_beta.rearrange("(a n) -> a n", a=1).broadcast_to([P, SEQ])),
                     (g_raw[:, 0:1], g_xattn.rearrange("(a n) -> a n", a=1).broadcast_to([P, 1])),
                     (g_raw[:, 1:2], g_ffn.rearrange("(a n) -> a n", a=1).broadcast_to([P, 1])),
                     (ebias[:, :], e_bias.rearrange("(a n) -> a n", a=1).broadcast_to([P, E])),
                     (gate[:, :, :], gate_w.rearrange("(h p) e -> p h e", p=P))]
            x_rows = x.rearrange("b (t p) n -> p (b t) n", p=P)
            ctx_rows = ctx_in.rearrange("b (t p) n -> p (b t) n", p=P)
            h_rows = h_dram.rearrange("(t p) n -> p t n", p=P)
            sp.dma_start(X[:, 0:TPB, :], x_rows[:, 0:TPB, :]).then_inc(s["d_x"], 16)
            sp.dma_start(ctx_b[:, :, :], ctx_rows[:, 0:TPB, :]).then_inc(s["d_ctx"], 16)
            for dst, src in small:
                sp.dma_start(dst, src).then_inc(s["d_small"], 16)
            sp.dma_start(wsu[:, :, :], w_sh_up.rearrange("(h p) n -> p h n", p=P)).then_inc(s["d_w"], 16)
            sp.dma_start(wsd[:, :, :], w_sh_down.rearrange("(k p) n -> p k n", p=P)).then_inc(s["d_w"], 16)
            with sp.Fori(1, N_BATCH) as b:
                wait(sp, "d_x", 16 * b)
                sp.dma_start(X[:, ds(TPB * b, TPB), :], x_rows[:, ds(TPB * b, TPB), :]).then_inc(s["d_x"], 16)
                wait(sp, "pe_ctxT", b)
                sp.dma_start(ctx_b[:, :, :], ctx_rows[:, ds(TPB * b, TPB), :]).then_inc(s["d_ctx"], 16)
                wait(sp, "dve_h", TPB * b)
                sp.dma_start(h_rows[:, ds(TPB * b - TPB, TPB), :], HR[:, :, :]).then_inc(s["d_h"], 16)
            wait(sp, "dve_h", NT)
            sp.dma_start(h_rows[:, NT - TPB:NT, :], HR[:, :, :]).then_inc(s["d_h"], 16)

            wu_rows = w_up.rearrange("e (h p) n -> p (e h) n", p=P)
            wd_rows = w_down.rearrange("e (k p) n -> p (e k) n", p=P)

            def load(e, slot):
                sp.dma_start(wu[:, slot, :, :], wu_rows[:, ds(e * HB, HB), :]).then_inc(d_wt[slot], 16)
                sp.dma_start(wd[:, slot, :, :], wd_rows[:, ds(e * IB, IB), :]).then_inc(d_wt[slot], 16)

            for e in range(W_SLOTS):
                load(e, e)
            for e in range(W_SLOTS - 1):
                sp.wait_ge(d_wt[e], 32)
                sp.sem_inc(s["sp_w"], 1)
            wait(sp, "dve_tab", 3)
            with sp.Fori(W_SLOTS, E - W_SLOTS + 1, W_SLOTS) as i:
                for j in range(W_SLOTS):
                    free_at = sp.value_load(done_tab[0:1, ds(i + (j - W_SLOTS), 1)], min_val=1, max_val=N_TILES + 1)
                    wait(sp, "pe_ed", free_at)
                    load(i + j, j)
                    before = (j - 1) % W_SLOTS
                    sp.wait_ge(d_wt[before], 8 * (i + (j - 1 - before)) + 32)
                    sp.sem_inc(s["sp_w"], 1)
            sp.wait_ge(d_wt[W_SLOTS - 1], 32 * (E // W_SLOTS))
            sp.sem_inc(s["sp_w"], 1)

            used = load_used(sp)
            y_groups = y_dram.rearrange("(t p) n -> p t n", p=P)
            with sp.Fori(NT * TOPK, N_TILES - UNROLL + 1, UNROLL) as i:
                with sp.If(i < used):
                    sp.sem_inc(s["d_fill"], 16)
                with sp.Else():
                    sp.dma_start(y_groups[:, ds(i, UNROLL), :], X[:, 0:UNROLL, :]).then_inc(s["d_fill"], 16)

            out_rows = out.rearrange("b (t p) n -> p (b t) n", p=P)
            with sp.Fori(0, NT) as t:
                wait(sp, "dve_cmb", TOPK * (t + 1))
                sp.dma_start(out_rows[:, ds(t, 1), :], X[:, ds(t, 1), :]).then_inc(s["d_out"], 16)
            wait(sp, "d_out", 16 * NT)

        @blk.gpsimd
        def _(pool):
            c = s["pool_c"]
            pool.memset(ident[:, :], 0.0).then_inc(c, 1)
            pool.memset(lower[:, :], 0.0).then_inc(c, 1)
            pool.memset(ones[:, :], 1.0).then_inc(c, 1)
            pool.memset(zeros[:, :], 0.0).then_inc(c, 1)
            pool.memset(mhalf[:, :], -0.5).then_inc(c, 1)
            pool.memset(lt44[:, :, :], 0.0).then_inc(c, 1)
            pool.memset(onesE[:, :], 1.0).then_inc(c, 1)
            pool.iota(iota_i[:, :], pattern=[[1, P]], base=0, channel_multiplier=0).then_inc(c, 1)
            pool.iota(part_i[:, :], pattern=[[0, 1]], base=0, channel_multiplier=1).then_inc(c, 1)
            pool.iota(tok_i[:, :], pattern=[[P, NT]], base=0, channel_multiplier=1).then_inc(c, 1)
            wait(pool, "pool_c", 10)
            pool.affine_select(out=ident[:, :], in_=ident[:, :], compare_op=ALU.not_equal, fill=1.0,
                               base=0, pattern=[[-1, P]], channel_multiplier=1).then_inc(c, 1)
            pool.affine_select(out=lower[:, :], in_=lower[:, :], compare_op=ALU.is_ge, fill=1.0,
                               base=0, pattern=[[-1, P]], channel_multiplier=1).then_inc(c, 1)
            pool.affine_select(out=lt44[:, :, :], in_=lt44[:, :, :], compare_op=ALU.is_ge, fill=1.0,
                               base=0, pattern=[[-1, GROUPS], [1, GROUPS]], channel_multiplier=0).then_inc(c, 1)
            pool.tensor_copy(iota_f[:, :], iota_i[:, :]).then_inc(c, 1)
            pool.tensor_copy(iota_h[:, :], iota_i[:, :]).then_inc(c, 1)
            pool.tensor_copy(part_f[:, :], part_i[:, :]).then_inc(c, 1)
            pool.tensor_copy(tok_f[:, :], tok_i[:, :]).then_inc(c, 1)
            pool.tensor_scalar(edge[:, :], iota_i[:, 0:NT], float(P), 0.0, ALU.mult, ALU.add).then_inc(c, 1)

            with pool.Fori(0, N_BATCH) as b:
                for j in range(3):
                    wait(pool, "dve_v", 3 * b + j + 1)
                    pool.tensor_tensor(rstd[:, j, :], veps[:, :], mhalf[:, :], ALU.pow).then_inc(s["pool_r"], 1)

            wait(pool, "dve_idx", 1)
            wait(pool, "d_h", 16 * N_BATCH)

            def gather(i, u, first):
                if not first:
                    wait_first(pool, "pe_xT", i + (u - UNROLL + 1))
                pool.tensor_copy(idx_now[:, u:u + 1], idx_g[:, ds(i + u, 1)]).then_inc(s["pool_idx"], 1)
                gate_pool(pool, s["pool_idx"], i + u + 1)
                pool.indirect_dma_start(out=xg[:, u, :], out_offset=None, in_=h_dram[:, :],
                                        in_offset=bass.IndirectOffsetOnAxis(ap=idx_now[:, u:u + 1], axis=0),
                                        bounds_check=NT * P - 1).then_inc(d_xg[u], 16)

            used = load_used(pool)
            for u in range(UNROLL):
                gather(0, u, True)
            with pool.Fori(UNROLL, N_TILES - UNROLL + 1, UNROLL) as i:
                with pool.If(i < used):
                    for u in range(UNROLL):
                        gather(i, u, False)

            stored = pool.value_load(used_tab[0:1, 1:2], min_val=16, max_val=16 * N_TILES // UNROLL)
            wait(pool, "d_fill", 16 * (N_TILES - NT * TOPK) // UNROLL)
            for u in range(UNROLL):
                gate_pool(pool, d_y[u], stored, 2 + u)

            def combine(t, first):
                for u in range(UNROLL):
                    if not first:
                        gate_pool(pool, s["dve_cmb"], TOPK * (t + (u + 1 - UNROLL)), 2 + UNROLL + u)
                    pool.tensor_copy(yidx[:, u * TOPK:(u + 1) * TOPK], s4i[:, ds((t + u) * TOPK, TOPK)])\
                        .then_inc(s["pool_cidx"], 1)
                    gate_pool(pool, s["pool_cidx"], t + u + 1, 1)
                    for k in range(TOPK):
                        at = u * TOPK + k
                        pool.indirect_dma_start(out=yg[:, u, k, :], out_offset=None, in_=y_dram[:, :],
                                                in_offset=bass.IndirectOffsetOnAxis(ap=yidx[:, at:at + 1], axis=0),
                                                bounds_check=N_TILES * P - 1).then_inc(d_yg[u], 16)

            combine(0, True)
            with pool.Fori(UNROLL, NT - UNROLL + 1, UNROLL) as t:
                combine(t, False)

        @blk.scalar
        def _(ac):
            def go(out_, in_, func, name, **kw):
                return ac.activation(out_, in_, func, **kw).then_inc(s[name], 1)

            wait(ac, "d_small", 16 * 8)
            go(g_tanh[:, :], g_raw[:, :], ACT.Tanh, "act_c")
            wait(ac, "pe_wk", 1)
            go(wkT[:, :], T[0][:, 0:DC], ACT.Copy, "act_c")

            def attend(b):
                wait(ac, "pe_ctxT", b + 1)
                go(ctxT[:, :], T[0][:, :], ACT.Copy, "act_ctxT")
                wait(ac, "pe_kvT", b + 1)
                go(kvT[:, :], U[0][:, :], ACT.Identity, "act_kvT", bias=bk[:, 0:1])
                for jb in (0, 2):
                    wait(ac, "pe_pT", TPB * b + jb + 1)
                    go(pT[:, jb, :], T[0][:, :], ACT.Copy, "act_pT")
                wait(ac, "pe_outT", b + 1)
                go(outT[:, :], U[1][:, :], ACT.Copy, "act_outT", scale=float(SEQ) ** -0.5)
                for it in range(TPB):
                    wait(ac, "pe_sim", TPB * b + it + 1)
                    go(PS[:, it, :], D[it][:, :], ACT.Copy, "act_sim")

            def relu(b, k):
                wait(ac, "pe_up", SB * b + k + 1)
                if k >= 2:
                    wait(ac, "dve_act", SB * b + k - 1)
                elif not (isinstance(b, int) and b == 0):
                    wait(ac, "dve_act", SB * b)
                go(rel[:, k % 2, :], U[k % 2][:, :], ACT.Relu, "act_r")

            def relu_last(k, odd=0):
                b = N_BATCH - 1
                wait(ac, "pe_up", k + (SB * b + 1))
                wait(ac, "dve_act", k + (SB * b - 1))
                go(rel[:, odd, :], U[odd][:, :], ACT.Relu, "act_r")

            def exps(b, it):
                wait(ac, "dve_z", TPB * b + it + 1)
                if it >= 2:
                    wait(ac, "dve_x1", TPB * b + it - 1)
                elif not (isinstance(b, int) and b == 0):
                    wait(ac, "dve_x1", TPB * b + it - 1)
                go(ex[:, it % 2, :], t2[:, it % 2, :], ACT.Exp, "act_e",
                   bias=nmax[:, it:it + 1], accum_out=esum[:, it:it + 1])

            def ends(b):
                slot = b % 2
                for it in (0, 2):
                    wait(ac, "pe_hT", TPB * b + it + 1)
                    dst = hT2[:, ds(slot * (HB * SEQ), HB * SEQ)].rearrange("p (h n) -> p h n", h=HB)
                    go(dst[:, :, it * P:(it + 1) * P], T[0][:, :].rearrange("p (h n) -> p h n", h=HB),
                       ACT.Copy, "act_hT")
                wait(ac, "pe_lgT", b + 1)
                go(lgT[:, :], U[0][0:E, :], ACT.Copy, "act_lgT")

            attend(0)
            for it in range(TPB):
                exps(0, it)
            ends(0)
            with ac.Fori(1, N_BATCH) as b:
                attend(b)
                for it in range(TPB):
                    exps(b, it)
                    relu(b - 1, 2 * it)
                    relu(b - 1, 2 * it + 1)
                ends(b)
            wait(ac, "dve_lg", N_BATCH)
            go(sc[:, :, :], LG[:, :, :], ACT.Sigmoid, "act_sc")

            def tile_in(i, u):
                wait(ac, "pe_xT", i + u + 1)
                go(xgT[:, u % 2, :, :], T[u % 2][:, :].rearrange("p (h n) -> p h n", h=HB), ACT.Copy, "act_xT")

            def tile_relu(i, u):
                wait(ac, "pe_eu", i + u + 1)
                go(erel[:, u % 2, :], U[u % 2][:, 0:INNER], ACT.Relu, "act_er")

            def store(i, u):
                wait(ac, "dve_y", i + u + 1)
                ac.dma_start(y_dram[ds((i + u) * P, P), :], yb[:, u, :]).then_inc(d_y[u], 16)

            used = load_used(ac)
            tile_in(0, 0)
            tile_relu(0, 0)
            tile_in(0, 1)

            def tiles(i, final=False):
                for u in range(UNROLL):
                    if u + 2 < UNROLL:
                        tile_in(i, u + 2)
                    elif not final:
                        with ac.If(i + UNROLL < used):
                            tile_in(i, u + 2)
                    if u + 1 < UNROLL:
                        tile_relu(i, u + 1)
                    elif not final:
                        with ac.If(i + UNROLL < used):
                            tile_relu(i, u + 1)
                    store(i, u)

            with ac.Fori(0, N_TILES - 2 * UNROLL + 1, UNROLL) as i:
                with ac.If(i < used):
                    tiles(i)
            with ac.If(used > N_TILES - UNROLL):
                tiles(N_TILES - UNROLL, final=True)
            with ac.Fori(0, SB - 1, 2) as k:
                relu_last(k)
                relu_last(k + 1, 1)

        @blk.vector
        def _(ve):
            chain = [0]

            def link(ins):
                chain[0] += 1
                ins.then_inc(s["dve_ch"], 1)
                wait(ve, "dve_ch", chain[0])

            ve.memset(pre[:, 0, :], 0.0).then_inc(s["dve_sh"], 1)
            wait(ve, "d_small", 16 * 8)
            wait(ve, "act_c", 1)

            STEPS = 40

            def batch(b, shared):
                first = isinstance(b, int) and b == 0
                n = [0]

                def step(ins):
                    n[0] += 1
                    ins.then_inc(s["dve_e"], 1)

                def settle(w=wait):
                    w(ve, "dve_e", STEPS * b + n[0])

                def Xt(it):
                    return X2[:, ds((TPB * b + it) * H, H)]

                def stats(src, eps, which):
                    for it in range(TPB):
                        step(ve.bn_stats(bst[:, it, :], src(it)))
                    settle()
                    ve.memset(gate_v[:, :], 0.0)
                    for it in range(TPB):
                        step(ve.bn_aggr(mv[:, it, :], bst[:, it, :]))
                    settle()
                    ve.tensor_scalar(veps[:, :], mv[:, :, 1], eps, None, ALU.add).then_inc(s["dve_v"], 1)
                    wait(ve, "pool_r", 3 * b + which + 1)

                wait_first(ve, "d_x", 16 * b + 16)
                stats(Xt, 1e-5, 0)
                for it in range(TPB):
                    ve.tensor_scalar(PS[:, it, :], Xt(it), mv[:, it, 0:1], rstd[:, 0, it:it + 1],
                                     ALU.subtract, ALU.mult).then_inc(s["dve_p"], 1)
                wait(ve, "pe_kv", b + 1)
                ve.tensor_copy(kv[:, :, :], T[1][:, :].rearrange("p (j d) -> p j d", d=DC)).then_inc(s["dve_kv"], 1)
                for jb in (1, 3):
                    wait(ve, "pe_pT", TPB * b + jb + 1)
                    ve.tensor_copy(pT[:, jb, :], T[1][:, :]).then_inc(s["dve_pT"], 1)
                wait_first(ve, "act_sim", TPB * b + TPB)
                stats(lambda it: PS[:, it, :], 1e-6, 1)
                for it in range(TPB):
                    step(ve.scalar_tensor_tensor(t1[:, it % 2, :], PS[:, it, :], mv[:, it, 0:1], gam[:, :],
                                                 ALU.subtract, ALU.mult))
                    settle()
                    if it >= 2:
                        wait(ve, "act_e", TPB * b + it - 1)
                    elif not first:
                        wait(ve, "act_e", TPB * b)
                    step(ve.scalar_tensor_tensor(t2[:, it % 2, :], t1[:, it % 2, :], rstd[:, 1, it:it + 1],
                                                 bet[:, :], ALU.mult, ALU.add))
                    settle()
                    ve.tensor_reduce(nmax[:, it:it + 1], t2[:, it % 2, :], AX.X, ALU.max,
                                     negate=True).then_inc(s["dve_z"], 1)
                    if shared:
                        square(b - 1, 2 * it)
                        square(b - 1, 2 * it + 1)
                    wait(ve, "act_e", TPB * b + it + 1)
                    step(ve.reciprocal(esum[:, it:it + 1], esum[:, it:it + 1]))
                    settle()
                    step(ve.tensor_tensor(ecoef[:, it:it + 1], esum[:, it:it + 1], g_tanh[:, 0:1], ALU.mult))
                    settle()
                    ve.scalar_tensor_tensor(Xt(it), ex[:, it % 2, :], ecoef[:, it:it + 1], Xt(it),
                                            ALU.mult, ALU.add).then_inc(s["dve_x1"], 1)
                wait_first(ve, "dve_x1", TPB * b + TPB)
                stats(Xt, 1e-5, 2)
                if not first:
                    wait(ve, "d_h", 16 * b)
                for it in range(TPB):
                    ve.tensor_scalar(HR[:, it, :], Xt(it), mv[:, it, 0:1], rstd[:, 2, it:it + 1],
                                     ALU.subtract, ALU.mult).then_inc(s["dve_h"], 1)
                if shared:
                    add_shared(b - 1)
                slot = b % 2
                for it in (1, 3):
                    wait(ve, "pe_hT", TPB * b + it + 1)
                    dst = hT2[:, ds(slot * (HB * SEQ), HB * SEQ)].rearrange("p (h n) -> p h n", h=HB)
                    ve.tensor_copy(dst[:, :, it * P:(it + 1) * P],
                                   T[1][:, :].rearrange("p (h n) -> p h n", h=HB)).then_inc(s["dve_hT"], 1)
                wait(ve, "pe_lg", b + 1)
                ve.tensor_copy(LG2[:, ds(b * (TPB * E), TPB * E)], U[1][:, 0:TPB * E]).then_inc(s["dve_lg"], 1)
                wait(ve, "dve_h", TPB * b + TPB)
                assert n[0] == STEPS, n

            def square(b, k):
                wait(ve, "act_r", SB * b + k + 1)
                if k >= 2:
                    wait(ve, "pe_down", SB * b + k - 1)
                elif not (isinstance(b, int) and b == 0):
                    wait(ve, "pe_down", SB * b)
                ve.scalar_tensor_tensor(act[:, k % 2, :], U[k % 2][:, :], 0.0, rel[:, k % 2, :],
                                        ALU.max, ALU.mult).then_inc(s["dve_act"], 1)

            def add_shared(b):
                wait(ve, "pe_down", SB * b + SB)
                for it in range(TPB):
                    xs = X2[:, ds((TPB * b + it) * H, H)]
                    ve.scalar_tensor_tensor(xs, D[it][:, :], g_tanh[:, 1:2], xs, ALU.mult, ALU.add)\
                      .then_inc(s["dve_sh"], 1)

            batch(0, False)
            with ve.Fori(1, N_BATCH) as b:
                batch(b, True)

            last = N_BATCH - 1
            wait(ve, "act_sc", 1)
            wait(ve, "pool_c", 18)
            grp = lambda t: t[:, :, :].rearrange("p t (g e) -> p (t g) e", e=EG)
            m1, cnt, m2, q, gs, gm = (gsm[:, j, :] for j in range(6))
            bc8 = lambda a: a.unsqueeze(2).broadcast_to([P, NT * GROUPS, EG])
            link(ve.tensor_tensor(sfc[:, :, :], sc[:, :, :], ebias[:, :].unsqueeze(1).broadcast_to([P, NT, E]), ALU.add))
            link(ve.tensor_reduce(m1, grp(sfc), AX.X, ALU.max))
            link(ve.tensor_tensor(grp(sm), grp(sfc), bc8(m1), ALU.is_equal))
            link(ve.tensor_reduce(cnt, grp(sm), AX.X, ALU.add))
            link(ve.scalar_tensor_tensor(sm[:, :, :], sm[:, :, :], FAR, sfc[:, :, :], ALU.mult, ALU.add))
            link(ve.tensor_reduce(m2, grp(sm), AX.X, ALU.max))
            link(ve.tensor_scalar(q, cnt, 2.0, FAR, ALU.is_lt, ALU.mult))
            link(ve.tensor_tensor(q, q, m1, ALU.add))
            link(ve.tensor_tensor(m2, m2, q, ALU.max))
            link(ve.tensor_tensor(gs, m1, m2, ALU.add))
            g3 = gs.rearrange("p (t g) -> p t g", g=GROUPS)
            other = g3.unsqueeze(2).broadcast_to([P, NT, GROUPS, GROUPS])
            own = g3.unsqueeze(3).broadcast_to([P, NT, GROUPS, GROUPS])
            link(ve.tensor_tensor(gcmp[:, 0, :, :, :], other, own, ALU.is_gt))
            link(ve.tensor_tensor(gcmp[:, 1, :, :, :], other, own, ALU.is_equal))
            link(ve.tensor_tensor(gcmp[:, 1, :, :, :], gcmp[:, 1, :, :, :],
                                  lt44[:, :, :].unsqueeze(1).broadcast_to([P, NT, GROUPS, GROUPS]), ALU.mult))
            link(ve.tensor_tensor(gcmp[:, 0, :, :, :], gcmp[:, 0, :, :, :], gcmp[:, 1, :, :, :], ALU.add))
            link(ve.tensor_reduce(gm, gcmp[:, 0, :, :, :].rearrange("p t g h -> p (t g) h"), AX.X, ALU.add))
            link(ve.tensor_scalar(gm, gm, float(TOP_GROUPS), None, ALU.is_lt))
            link(ve.tensor_tensor(grp(sm), grp(sfc), bc8(gm), ALU.mult))
            for t in range(NT):
                ve.max(top8[:, t, :], sm[:, t, :]).then_inc(s["dve_ch"], 1)
            chain[0] += NT
            wait(ve, "dve_ch", chain[0])
            for t in range(NT):
                ve.max_index(idx8[:, t, :], top8[:, t, :], sm[:, t, :]).then_inc(s["dve_ch"], 1)
            chain[0] += NT
            wait(ve, "dve_ch", chain[0])
            link(ve.tensor_copy(idxf[:, :, :], idx8[:, :, 0:TOPK]))
            o3 = oneh[:, :, :, :].rearrange("p t k e -> p (t k) e")
            t3 = tmp[:, :, :, :].rearrange("p t k e -> p (t k) e")
            link(ve.tensor_tensor(o3, iota_f[:, 0:E].unsqueeze(1).broadcast_to([P, NT * TOPK, E]),
                                  idxf[:, :, :].rearrange("p t k -> p (t k)").unsqueeze(2)
                                  .broadcast_to([P, NT * TOPK, E]), ALU.is_equal))
            with nc.allow_low_precision("sums are 0 or 1"):
                ve.tensor_reduce(chosen[:, :, :], oneh[:, :, :, :].rearrange("p t k e -> p t e k"), AX.X, ALU.add)\
                  .then_inc(s["dve_M"], 1)
            byk = lambda t: t.unsqueeze(2).broadcast_to([P, NT, TOPK, E])
            link(ve.tensor_tensor(tmp[:, :, :, :], oneh[:, :, :, :], byk(sc[:, :, :]), ALU.mult))
            link(ve.tensor_reduce(w4[:, :], t3, AX.X, ALU.add))
            w3 = w4[:, :].rearrange("p (t k) -> p t k", k=TOPK)
            link(ve.tensor_reduce(wsum[:, :], w3, AX.X, ALU.add))
            link(ve.tensor_scalar(wsum[:, :], wsum[:, :], 1e-20, None, ALU.add))
            link(ve.reciprocal(wsum[:, :], wsum[:, :]))
            link(ve.tensor_tensor(w3, w3, wsum[:, :].unsqueeze(2).broadcast_to([P, NT, TOPK]), ALU.mult))
            link(ve.tensor_scalar(w4[:, :], w4[:, :], SCALE, g_tanh[:, 1:2], ALU.mult, ALU.mult))
            wait(ve, "pe_rank", 1)
            for t in range(NT):
                link(ve.tensor_tensor(pre[:, t + 1, :], pre[:, t, :], T[1][:, t * E:(t + 1) * E], ALU.add))
            c3 = tmp[:, 0:NT // TOPK, :, :].rearrange("p t k e -> p (t k e)").rearrange("p (e j) -> p e j", e=E)
            link(ve.tensor_tensor(c3, pre[:, NT, :].unsqueeze(2).broadcast_to([P, E, NT]),
                                  edge[:, :].unsqueeze(1).broadcast_to([P, E, NT]), ALU.is_gt))
            link(ve.tensor_reduce(n_tl[:, :], c3, AX.X, ALU.add))
            link(ve.tensor_tensor_scan(tend[:, :], onesE[:, :], n_tl[:, :], 0.0, ALU.mult, ALU.add))
            ve.tensor_copy(used_tab[0:1, 0:1], tend[0:1, E - 1:E]).then_inc(s["dve_tab"], 1)
            link(ve.tensor_scalar(eid[0:1, 2:3], tend[0:1, E - 1:E], float(UNROLL - 1), None, ALU.add))
            link(ve.tensor_copy(eid_i[0:1, 0:1], eid[0:1, 2:3]))
            link(ve.tensor_scalar(used_tab[0:1, 1:2], eid_i[0:1, 0:1], 2, 4, ALU.logical_shift_right,
                                  ALU.logical_shift_left))
            ve.tensor_scalar(done_tab[0:1, :], tend[0:1, :], 1.0, None, ALU.add).then_inc(s["dve_tab"], 1)
            link(ve.tensor_tensor(base[:, :], tend[:, :], n_tl[:, :], ALU.subtract))
            link(ve.tensor_scalar(base[:, :], base[:, :], float(P), None, ALU.mult))
            p16 = pre[:, 0:NT, :]
            link(ve.tensor_tensor(p16, T[0][:, :].rearrange("p (t e) -> p t e", e=E), p16, ALU.add))
            link(ve.tensor_tensor(p16, p16, base[:, :].unsqueeze(1).broadcast_to([P, NT, E]), ALU.add))
            link(ve.tensor_scalar(onesE[:, :], tend[:, :], part_f[:, 0:1], None, ALU.is_le, ALU.add,
                                  accum_out=eid[:, 0:1]))
            link(ve.tensor_scalar(eid[:, 0:1], eid[:, 0:1], float(E - 1), None, ALU.min))
            link(ve.tensor_copy(eid_i[:, 0:1], eid[:, 0:1]))
            link(ve.tensor_scalar(eid_i[:, 1:2], eid_i[:, 0:1], W_SLOTS - 1, None, ALU.bitwise_and))
            link(ve.tensor_copy(eid[:, 1:2], eid_i[:, 1:2]))
            ve.tensor_scalar(eid[:, 0:1], eid[:, 0:1], 1.0, None, ALU.add).then_inc(s["dve_tabT"], 1)
            link(ve.tensor_tensor(tmp[:, :, :, :], oneh[:, :, :, :], byk(p16), ALU.mult))
            link(ve.tensor_reduce(s4[:, :], t3, AX.X, ALU.add))
            link(ve.tensor_copy(s4i[:, :], s4[:, :]))
            link(ve.tensor_scalar(sp_i[:, 0, :], s4i[:, :], P - 1, None, ALU.bitwise_and))
            link(ve.tensor_scalar(sp_i[:, 1, :], s4i[:, :], 7, None, ALU.logical_shift_right))
            link(ve.tensor_copy(sp_f[:, :, :], sp_i[:, :, :]))
            spf2 = sp_f[:, :, :].rearrange("p a n -> p (a n)")
            with ve.Fori(0, NT - 1, 2) as t:
                for u in range(2):
                    wait(ve, "pe_sel", t + u + 1)
                    for k in range(TOPK):
                        at = (t + u) * TOPK + k
                        ve.tensor_scalar(selA[:, u, k, :], iota_h[:, :], spf2[:, ds(at, 1)], None, ALU.is_equal)\
                          .then_inc(s["dve_sel"], 1)
                        ve.tensor_scalar(selB[:, u, k, :], iota_h[:, 0:N_TILES], spf2[:, ds(at + NT * TOPK, 1)],
                                         tok_f[:, ds(t + u, 1)], ALU.is_equal, ALU.mult)\
                          .then_inc(s["dve_sel"], 1)
            wait(ve, "pe_tab", 1)
            ve.tensor_copy(tab[0:1, :], U[1][0:1, 0:2 * P]).then_inc(s["dve_tab"], 1)
            wait(ve, "pe_ix", 1)
            ve.tensor_copy(idx_g[:, :], T[0][:, 0:N_TILES]).then_inc(s["dve_idx"], 1)

            def tile_square(i, u):
                wait(ve, "act_er", i + u + 1)
                ve.scalar_tensor_tensor(eact[:, u % 2, :], U[u % 2][:, 0:INNER], 0.0, erel[:, u % 2, :],
                                        ALU.max, ALU.mult).then_inc(s["dve_eact"], 1)

            def tile_actT(i, u):
                wait(ve, "pe_eT", i + u + 1)
                ve.tensor_copy(eactT[:, u % 2, :, :],
                               D[u % 2][:, 0:INNER].rearrange("p (k n) -> p k n", k=IB)).then_inc(s["dve_eT"], 1)

            def tile_out(i, u, first):
                wait(ve, "pe_ed", i + u + 2)
                if not first:
                    ve.wait_ge(d_y[u], 4 * i)
                ve.tensor_copy(yb[:, u, :], D[2 + u % 2][:, :]).then_inc(s["dve_y"], 1)

            used = load_used(ve)
            tile_square(0, 0)

            def tiles(i, first=False, final=False):
                for u in range(UNROLL):
                    tile_actT(i, u)
                    if u + 1 < UNROLL:
                        tile_square(i, u + 1)
                    elif not final:
                        with ve.If(i + UNROLL < used):
                            tile_square(i, u + 1)
                    tile_out(i, u, first)

            tiles(0, first=True)
            with ve.Fori(UNROLL, N_TILES - 2 * UNROLL + 1, UNROLL) as i:
                with ve.If(i < used):
                    tiles(i)
            with ve.If(used > N_TILES - UNROLL):
                tiles(N_TILES - UNROLL, final=True)
            ve.memset(gate_v[:, :], 0.0).then_inc(s["dve_done"], 1)

            def combine(t, u):
                ve.wait_ge(d_yg[u], 4 * TOPK * t + 16 * TOPK)
                xs = X2[:, ds((t + u) * H, H)]
                for k in range(TOPK):
                    w = w4[:, ds((t + u) * TOPK + k, 1)]
                    if k:
                        wait(ve, "dve_cmb", TOPK * (t + u) + k)
                    ve.scalar_tensor_tensor(xs, yg[:, u, k, :], w, xs, ALU.mult, ALU.add)\
                      .then_inc(s["dve_cmb"], 1)

            def square_last(k, odd):
                b = N_BATCH - 1
                wait(ve, "act_r", k + (SB * b + 1))
                wait(ve, "pe_down", k + (SB * b - 1))
                ve.scalar_tensor_tensor(act[:, odd, :], U[odd][:, :], 0.0, rel[:, odd, :],
                                        ALU.max, ALU.mult).then_inc(s["dve_act"], 1)

            square_last(0, 0)
            square_last(1, 1)
            with ve.Fori(0, NT - 2 * UNROLL + 1, UNROLL) as t:
                for u in range(UNROLL):
                    combine(t, u)
                    if u % 2:
                        continue
                    square_at = [t // 2 + 2, t // 2 + 3][u // 2]
                    square_last(square_at, u // 2)
            wait(ve, "dve_cmb", TOPK * (NT - UNROLL))
            add_shared(last)
            wait(ve, "dve_sh", 1 + NT)
            for u in range(UNROLL):
                combine(NT - UNROLL, u)

        @blk.tensor
        def _(pe):
            def mm(o, l, r, start=True, stop=True):
                return pe.matmul(o, l, r, start=start, stop=stop)

            wait(pe, "d_small", 16 * 8)
            wait(pe, "pool_c", 18)
            pe.transpose(T[0][:, 0:DC], wk[:, :], ident[:, :]).then_inc(s["pe_wk"], 1)
            wait(pe, "act_c", 2)

            def attend(b):
                first = isinstance(b, int) and b == 0
                wait(pe, "d_ctx", 16 * b + 16)
                if not first:
                    wait(pe, "act_hT", 2 * b)
                for j in range(TPB):
                    i_ = pe.transpose(T[0][:, j * P:(j + 1) * P], ctx_b[:, j, :], ident[:, :])
                i_.then_inc(s["pe_ctxT"], 1)
                wait(pe, "act_ctxT", b + 1)
                if not first:
                    wait(pe, "act_lgT", b)
                mm(U[0][:, :], wkT[:, :], ctxT[:, :]).then_inc(s["pe_kvT"], 1)
                wait(pe, "act_kvT", b + 1)
                if not first:
                    wait(pe, "dve_hT", 2 * b)
                for j in range(TPB):
                    i_ = pe.transpose(T[1][:, j * P:(j + 1) * P], kvT[:, j * P:(j + 1) * P], ident[:, :])
                i_.then_inc(s["pe_kv"], 1)
                wait(pe, "dve_p", TPB * b + TPB)

                def p_block(j):
                    for it in range(TPB):
                        i_ = pe.transpose(T[j % 2][:, it * P:(it + 1) * P], PS[:, it, j * P:(j + 1) * P], ident[:, :])
                    i_.then_inc(s["pe_pT"], 1)

                def o_block(j):
                    return mm(U[1][:, :], kv[:, j, :], pT[:, j, :], j == 0, j == TPB - 1)

                p_block(0)
                wait(pe, "dve_kv", b + 1)
                p_block(1)
                wait(pe, "act_pT", 2 * b + 1)
                p_block(2)
                if not first:
                    wait(pe, "dve_lg", b)
                o_block(0)
                wait(pe, "dve_pT", 2 * b + 1)
                p_block(3)
                o_block(1)
                wait(pe, "act_pT", 2 * b + 2)
                o_block(2)
                wait(pe, "dve_pT", 2 * b + 2)
                o_block(3).then_inc(s["pe_outT"], 1)
                wait(pe, "act_outT", b + 1)
                if not first:
                    wait(pe, "dve_sh", TPB * b - TPB + 1)
                for it in range(TPB):
                    mm(D[it][:, :], outT[:, it * P:(it + 1) * P], kvT[:, :]).then_inc(s["pe_sim"], 1)

            def shared_up(b, k):
                slot = b % 2
                for h in range(HB):
                    i_ = mm(U[k % 2][:, :], wsu[:, h, k * P:(k + 1) * P],
                            hT2[:, ds((slot * HB + h) * SEQ, SEQ)], h == 0, h == HB - 1)
                i_.then_inc(s["pe_up"], 1)

            def shared_down(b, k):
                wait(pe, "dve_act", SB * b + k + 1)
                for it in range(TPB):
                    i_ = mm(D[it][:, :], act[:, k % 2, it * P:(it + 1) * P], wsd[:, k, :], k == 0, k == SB - 1)
                i_.then_inc(s["pe_down"], 1)

            def shared(b, ks):
                for k in ks:
                    if k == 0:
                        shared_up(b, 0)
                    if k + 1 < SB:
                        shared_up(b, k + 1)
                    shared_down(b, k)

            def ends(b):
                first = isinstance(b, int) and b == 0
                for it in range(TPB):
                    wait(pe, "dve_h", TPB * b + it + 1)
                    if it < 2:
                        wait(pe, ("act_pT", "dve_pT")[it], 2 * b + 2)
                    else:
                        wait(pe, ("act_hT", "dve_hT")[it - 2], 2 * b + 1)
                    for h in range(HB):
                        i_ = pe.transpose(T[it % 2][:, h * P:(h + 1) * P], HR[:, it, h * P:(h + 1) * P], ident[:, :])
                    i_.then_inc(s["pe_hT"], 1)
                wait(pe, "act_hT", 2 * b + 2)
                wait(pe, "dve_hT", 2 * b + 2)
                if not first:
                    wait(pe, "dve_act", SB * b)
                slot = b % 2
                for h in range(HB):
                    i_ = mm(U[0][0:E, :], gate[:, h, :], hT2[:, ds((slot * HB + h) * SEQ, SEQ)], h == 0, h == HB - 1)
                i_.then_inc(s["pe_lgT"], 1)
                wait_first(pe, "act_lgT", b + 1)
                for it in range(TPB):
                    i_ = pe.transpose(U[1][:, it * E:(it + 1) * E], lgT[:, it * P:(it + 1) * P], ident[0:E, 0:E])
                i_.then_inc(s["pe_lg"], 1)

            attend(0)
            ends(0)
            wait(pe, "d_w", 32)
            with pe.Fori(1, N_BATCH) as b:
                attend(b)
                wait(pe, "act_sim", TPB * b + TPB)
                shared(b - 1, range(SB))
                ends(b)
            wait(pe, "dve_M", 1)
            ch = chosen[:, :, :].rearrange("p t e -> p (t e)")
            mm(T[0][:, :], lower[:, :], ch)
            mm(T[1][:, :], ones[:, :], ch).then_inc(s["pe_rank"], 1)
            wait(pe, "dve_lg", N_BATCH)
            wait(pe, "dve_tabT", 1)
            for j in range(2):
                i_ = pe.transpose(U[1][0:1, j * P:(j + 1) * P], eid[:, j:j + 1], ident[:, :])
            i_.then_inc(s["pe_tab"], 1)
            pe.sem_inc(s["pe_sel"], 2)
            wait(pe, "dve_sel", 2 * TOPK)
            mm(T[0][:, 0:N_TILES], zeros[:, :], zeros[:, 0:N_TILES], True, False)
            with pe.Fori(0, NT - 1, 2) as t:
                for u in range(2):
                    wait(pe, "dve_sel", 2 * TOPK * (t + u + 1))
                    for k in range(TOPK):
                        i_ = mm(T[0][:, 0:N_TILES], selA[:, u, k, :], selB[:, u, k, :], False, False)
                    i_.then_inc(s["pe_sel"], 1)
            mm(T[0][:, 0:N_TILES], zeros[:, :], zeros[:, 0:N_TILES], False, True).then_inc(s["pe_ix"], 1)

            used = load_used(pe)
            wait(pe, "dve_sh", 1 + TPB * (N_BATCH - 1))

            def rows(i, u):
                pe.wait_ge(d_xg[u % UNROLL], 4 * (i + (u - u % UNROLL)) + 16)
                for h in range(HB):
                    i_ = pe.transpose(T[u % 2][:, h * P:(h + 1) * P], xg[:, u % UNROLL, h * P:(h + 1) * P], ident[:, :])
                i_.then_inc(s["pe_xT"], 1)

            def w_ready(i, u):
                return pe.value_load(tab[0:1, ds(i + u, 1)], min_val=1, max_val=E)

            def w_slot(i, u):
                return pe.value_load(tab[0:1, ds(i + (u + P), 1)], min_val=0, max_val=W_SLOTS - 1)

            def up(i, u, ready, slot):
                wait(pe, "sp_w", ready)
                wait(pe, "act_xT", i + (u + 1))
                for h in range(HB):
                    i_ = mm(U[u % 2][:, 0:INNER], xgT[:, u % 2, h, :],
                            wu2[:, ds((slot * HB + h) * INNER, INNER)], h == 0, h == HB - 1)
                i_.then_inc(s["pe_eu"], 1)

            def act_t(i, u):
                wait(pe, "dve_eact", i + (u + 1))
                for k in range(IB):
                    i_ = pe.transpose(D[u % 2][:, k * P:(k + 1) * P], eact[:, u % 2, k * P:(k + 1) * P], ident[:, :])
                i_.then_inc(s["pe_eT"], 1)

            def down(i, u, slot):
                wait(pe, "dve_eT", i + (u + 1))
                for k in range(IB):
                    i_ = mm(D[2 + u % 2][:, :], eactT[:, u % 2, k, :],
                            wd2[:, ds((slot * IB + k) * H, H)], k == 0, k == IB - 1)
                i_.then_inc(s["pe_ed"], 1)

            pe.sem_inc(s["pe_ed"], 1)
            rows(0, 0)
            up(0, 0, w_ready(0, 0), w_slot(0, 0))
            rows(0, 1)

            def tiles(i, final=False):
                for u in range(UNROLL):
                    slot = w_slot(i, u)
                    inside = u + 1 < UNROLL
                    if inside or not final:
                        ready, slot_next = w_ready(i, u + 1), w_slot(i, u + 1)
                    act_t(i, u)
                    if u + 2 < UNROLL:
                        rows(i, u + 2)
                    elif not final:
                        with pe.If(i + UNROLL < used):
                            rows(i, u + 2)
                    if inside:
                        up(i, u + 1, ready, slot_next)
                    elif not final:
                        with pe.If(i + UNROLL < used):
                            up(i, u + 1, ready, slot_next)
                    down(i, u, slot)

            with pe.Fori(0, N_TILES - 2 * UNROLL + 1, UNROLL) as i:
                with pe.If(i < used):
                    tiles(i)
            with pe.If(used > N_TILES - UNROLL):
                tiles(N_TILES - UNROLL, final=True)
            wait(pe, "dve_done", 1)
            shared(N_BATCH - 1, range(SB))


_INS = ["x", "ctx_512", "g_xattn", "g_ffn", "L0_xattn_W_k", "L0_xattn_b_k", "L0_xattn_ln_gamma",
        "L0_xattn_ln_beta", "L0_ffn_gate_w", "L0_ffn_e_bias", "L0_ffn_Wu", "L0_ffn_Wd", "L0_ffn_Wsu",
        "L0_ffn_Wsd"]


def kernel(**inputs):
    import numpy as np
    import concourse.bacc as bacc
    from concourse.bass_utils import run_bass_kernel_spmd

    nc = bacc.Bacc("TRN2", target_bir_lowering=False, num_devices=1)
    arrays, args = {}, []
    for name in _INS:
        a = np.ascontiguousarray(inputs[name])
        arrays[f"in_{name}"] = a
        args.append(nc.dram_tensor(f"in_{name}", a.shape, mybir.dt.from_np(a.dtype), kind="ExternalInput").ap())
    out = nc.dram_tensor("out", inputs["x"].shape, mybir.dt.float32, kind="ExternalOutput").ap()
    block_kernel(nc, *args, out)
    r = run_bass_kernel_spmd(nc, [arrays], core_ids=[0])
    return r.results[0]["out"]
```
